# Optimizing a Trainium2 kernel written in Bass

```python
import numpy as np
import jax
import jax.numpy as jnp

def _softmax(x, axis=-1):
    return jax.nn.softmax(x, axis=axis)

def _gelu(x):
    return jax.nn.gelu(x, approximate=True)

def _silu(x):
    return jax.nn.silu(x)

def _sigmoid(x):
    return jax.nn.sigmoid(x)

def _layernorm(x, axis=-1, eps=1e-05):
    m = jnp.mean(x, axis=axis, keepdims=True)
    v = jnp.var(x, axis=axis, keepdims=True)
    return (x - m) / jnp.sqrt(v + eps)

def _scatter_add(tgt, idx, src, axis=0):
    return tgt.at[idx].add(src)

def _segment_sum(src, seg, n):
    return jax.ops.segment_sum(src, seg, n)
kernel_name = 'mk_audio_tower_d1_tok_audfeat512_r4_d1804e'

def setup_inputs(seed: int=0):
    np.random.seed(seed)
    _w = jnp.asarray

    def _rec_inputs():
        import jax
        import jax.numpy as jnp
        _rk = jax.random.key(seed)
        x = 7.22013e-05 + 1.00017 * jax.random.normal(jax.random.fold_in(_rk, 1), (32, 750, 128), jnp.float32)
        return x
    x = _rec_inputs()

    def _L0_tok_setup():
        import jax, jax.numpy as jnp
        import numpy as np
        H = 8
        TOP_FRAC = 0.2
        EPS = 1e-05

        def _layernorm(x, g, b):
            mu = jnp.mean(x, axis=-1, keepdims=True)
            var = jnp.mean((x - mu) ** 2, axis=-1, keepdims=True)
            return (x - mu) * jax.lax.rsqrt(var + EPS) * g + b
        key = jax.random.key(seed)
        ks = jax.random.split(key, 8)
        B, L, D, F = (8, 512, 128, 512)
        s = 0.02
        return {'x': jax.random.normal(ks[0], (B, L, D), jnp.float32), 'q_w': jax.random.normal(ks[1], (D, D), jnp.float32) * s, 'q_b': jnp.zeros((D,), jnp.float32), 'k_w': jax.random.normal(ks[2], (D, D), jnp.float32) * s, 'k_b': jnp.zeros((D,), jnp.float32), 'v_w': jax.random.normal(ks[3], (D, D), jnp.float32) * s, 'v_b': jnp.zeros((D,), jnp.float32), 'o_w': jax.random.normal(ks[4], (D, D), jnp.float32) * s, 'o_b': jnp.zeros((D,), jnp.float32), 'ln1_g': jnp.ones((D,), jnp.float32), 'ln1_b': jnp.zeros((D,), jnp.float32), 'f1_w': jax.random.normal(ks[5], (D, F), jnp.float32) * s, 'f1_b': jnp.zeros((F,), jnp.float32), 'f2_w': jax.random.normal(ks[6], (F, D), jnp.float32) * s, 'f2_b': jnp.zeros((D,), jnp.float32), 'ln2_g': jnp.ones((D,), jnp.float32), 'ln2_b': jnp.zeros((D,), jnp.float32), 'conv_w': jax.random.normal(ks[7], (D, D, 3), jnp.float32) * s, 'conv_b': jnp.zeros((D,), jnp.float32)}
    _L0_tok_all = _L0_tok_setup()
    _L0_tok_in = {k: v for k, v in _L0_tok_all.items() if k in ('q_w', 'q_b', 'k_w', 'k_b', 'v_w', 'v_b', 'o_w', 'o_b', 'ln1_g', 'ln1_b', 'f1_w', 'f1_b', 'f2_w', 'f2_b', 'ln2_g', 'ln2_b', 'conv_w', 'conv_b')}
    del _L0_tok_all

    def _L0_attn_setup():
        import jax, jax.numpy as jnp
        import numpy as np
        B, T, D, DS, EXP = (1, 512, 128, 32, 2)
        EPS = 1e-06

        def _ssm_scan(xs, dt, Bm, Cm, A):
            log_a = jnp.clip(dt * A[None, None, :], -20.0, 20.0)
            cum = jnp.cumsum(log_a, axis=1)
            dtx = dt * xs
            inp = dtx[..., None] * Bm[:, :, None, :]
            scaled = jnp.exp(-cum)[..., None] * inp
            prefix = jnp.cumsum(scaled, axis=1)
            h_all = jnp.exp(cum)[..., None] * prefix
            return jnp.einsum('btds,bts->btd', h_all, Cm)

        def _forward(x, norm_w, W_in, conv_w, conv_b, W_dt, b_dt, W_B, W_C, W_out, log_A, D_param, W_ffn1, W_ffn2, W_merge):
            r = x
            rms = jnp.sqrt(jnp.mean(x * x, axis=-1, keepdims=True) + EPS)
            xn = x / rms * norm_w
            xz = xn @ W_in
            xs, z = jnp.split(xz, 2, axis=-1)
            xt = jnp.transpose(xs, (0, 2, 1))
            c = jax.lax.conv_general_dilated(xt, conv_w, window_strides=(1,), padding=[(3, 0)], feature_group_count=D, dimension_numbers=('NCH', 'OIH', 'NCH'))
            c = c + conv_b[None, :, None]
            xs = jax.nn.silu(jnp.transpose(c, (0, 2, 1)))
            dt = jax.nn.softplus(xs @ W_dt + b_dt)
            Bm = xs @ W_B
            Cm = xs @ W_C
            A = -jnp.exp(log_A)
            y = _ssm_scan(xs, dt, Bm, Cm, A)
            y_ssm = (y + xs * D_param) * jax.nn.silu(z)
            y_ssm = y_ssm @ W_out
            y_ffn = jax.nn.gelu(xn @ W_ffn1, approximate=False) @ W_ffn2
            y = jnp.concatenate([y_ssm, y_ffn], axis=-1) @ W_merge
            return r + y
        key = jax.random.key(seed)
        ks = jax.random.split(key, 16)
        g = lambda k, shape, s: jax.random.normal(k, shape, jnp.float32) * s
        x = jax.random.normal(ks[0], (B, T, D), jnp.float32)
        inv = D ** (-0.5)
        return {'x': x, 'norm_w': jnp.ones((D,), jnp.float32), 'W_in': g(ks[1], (D, 2 * D), inv), 'conv_w': g(ks[2], (D, 1, 4), 0.5), 'conv_b': g(ks[3], (D,), 0.1), 'W_dt': g(ks[4], (D, D), 0.01 * inv), 'b_dt': jnp.full((D,), -8.0, jnp.float32) + g(ks[5], (D,), 0.1), 'W_B': g(ks[6], (D, DS), inv), 'W_C': g(ks[7], (D, DS), inv), 'W_out': g(ks[8], (D, D), inv), 'log_A': jnp.log(jnp.linspace(1.0, 16.0, D)).astype(jnp.float32), 'D_param': jnp.ones((D,), jnp.float32), 'W_ffn1': g(ks[9], (D, EXP * D), inv), 'W_ffn2': g(ks[10], (EXP * D, D), (EXP * D) ** (-0.5)), 'W_merge': g(ks[11], (2 * D, D), (2 * D) ** (-0.5))}
    _L0_attn_all = _L0_attn_setup()
    _L0_attn_in = {k: v for k, v in _L0_attn_all.items() if k in ('norm_w', 'W_in', 'conv_w', 'conv_b', 'W_dt', 'b_dt', 'W_B', 'W_C', 'W_out', 'log_A', 'D_param', 'W_ffn1', 'W_ffn2', 'W_merge')}
    del _L0_attn_all

    def _L0_ffn_setup():
        import jax, jax.numpy as jnp
        import numpy as np
        CAPACITY_FACTOR = 1.2
        key = jax.random.key(seed)
        k1, k2, k3 = jax.random.split(key, 3)
        B, S, D, E = (8, 1024, 128, 16)
        x = jax.random.normal(k1, (B, S, D), dtype=jnp.float32)
        switch_w = jax.random.normal(k2, (E, D), dtype=jnp.float32) * 0.02
        switch_b = jnp.zeros((E,), dtype=jnp.float32)
        expert_w = jax.random.normal(k3, (E, D, D), dtype=jnp.float32) * 0.02
        expert_b = jnp.zeros((E, D), dtype=jnp.float32)
        return {'x': x, 'switch_w': switch_w, 'switch_b': switch_b, 'expert_w': expert_w, 'expert_b': expert_b}
    _L0_ffn_all = _L0_ffn_setup()
    _L0_ffn_in = {k: v for k, v in _L0_ffn_all.items() if k in ('switch_w', 'switch_b', 'expert_w', 'expert_b')}
    del _L0_ffn_all
    return {'x': x, 'L0_tok_q_w': _L0_tok_in['q_w'], 'L0_tok_q_b': _L0_tok_in['q_b'], 'L0_tok_k_w': _L0_tok_in['k_w'], 'L0_tok_k_b': _L0_tok_in['k_b'], 'L0_tok_v_w': _L0_tok_in['v_w'], 'L0_tok_v_b': _L0_tok_in['v_b'], 'L0_tok_o_w': _L0_tok_in['o_w'], 'L0_tok_o_b': _L0_tok_in['o_b'], 'L0_tok_ln1_g': _L0_tok_in['ln1_g'], 'L0_tok_ln1_b': _L0_tok_in['ln1_b'], 'L0_tok_f1_w': _L0_tok_in['f1_w'], 'L0_tok_f1_b': _L0_tok_in['f1_b'], 'L0_tok_f2_w': _L0_tok_in['f2_w'], 'L0_tok_f2_b': _L0_tok_in['f2_b'], 'L0_tok_ln2_g': _L0_tok_in['ln2_g'], 'L0_tok_ln2_b': _L0_tok_in['ln2_b'], 'L0_tok_conv_w': _L0_tok_in['conv_w'], 'L0_tok_conv_b': _L0_tok_in['conv_b'], 'L0_attn_norm_w': _L0_attn_in['norm_w'], 'L0_attn_W_in': _L0_attn_in['W_in'], 'L0_attn_conv_w': _L0_attn_in['conv_w'], 'L0_attn_conv_b': _L0_attn_in['conv_b'], 'L0_attn_W_dt': _L0_attn_in['W_dt'], 'L0_attn_b_dt': _L0_attn_in['b_dt'], 'L0_attn_W_B': _L0_attn_in['W_B'], 'L0_attn_W_C': _L0_attn_in['W_C'], 'L0_attn_W_out': _L0_attn_in['W_out'], 'L0_attn_log_A': _L0_attn_in['log_A'], 'L0_attn_D_param': _L0_attn_in['D_param'], 'L0_attn_W_ffn1': _L0_attn_in['W_ffn1'], 'L0_attn_W_ffn2': _L0_attn_in['W_ffn2'], 'L0_attn_W_merge': _L0_attn_in['W_merge'], 'L0_ffn_switch_w': _L0_ffn_in['switch_w'], 'L0_ffn_switch_b': _L0_ffn_in['switch_b'], 'L0_ffn_expert_w': _L0_ffn_in['expert_w'], 'L0_ffn_expert_b': _L0_ffn_in['expert_b']}

def reference(x, L0_tok_q_w, L0_tok_q_b, L0_tok_k_w, L0_tok_k_b, L0_tok_v_w, L0_tok_v_b, L0_tok_o_w, L0_tok_o_b, L0_tok_ln1_g, L0_tok_ln1_b, L0_tok_f1_w, L0_tok_f1_b, L0_tok_f2_w, L0_tok_f2_b, L0_tok_ln2_g, L0_tok_ln2_b, L0_tok_conv_w, L0_tok_conv_b, L0_attn_norm_w, L0_attn_W_in, L0_attn_conv_w, L0_attn_conv_b, L0_attn_W_dt, L0_attn_b_dt, L0_attn_W_B, L0_attn_W_C, L0_attn_W_out, L0_attn_log_A, L0_attn_D_param, L0_attn_W_ffn1, L0_attn_W_ffn2, L0_attn_W_merge, L0_ffn_switch_w, L0_ffn_switch_b, L0_ffn_expert_w, L0_ffn_expert_b):
    import jax
    import jax.numpy as jnp

    def _L0_tok_ref(x, q_w, q_b, k_w, k_b, v_w, v_b, o_w, o_b, ln1_g, ln1_b, f1_w, f1_b, f2_w, f2_b, ln2_g, ln2_b, conv_w, conv_b):
        import jax, jax.numpy as jnp
        import numpy as np
        H = 8
        TOP_FRAC = 0.2
        EPS = 1e-05

        def _layernorm(x, g, b):
            mu = jnp.mean(x, axis=-1, keepdims=True)
            var = jnp.mean((x - mu) ** 2, axis=-1, keepdims=True)
            return (x - mu) * jax.lax.rsqrt(var + EPS) * g + b
        B, L, D = x.shape
        hd = D // H
        scale = hd ** (-0.5)
        k_top = max(1, int(L * TOP_FRAC))

        def split_heads(t):
            return t.reshape(B, L, H, hd).transpose(0, 2, 1, 3)
        q = split_heads(x @ q_w + q_b)
        k = split_heads(x @ k_w + k_b)
        v = split_heads(x @ v_w + v_b)
        q_norm = jnp.sum(q * q, axis=-1)
        _, top_idx = jax.lax.top_k(q_norm, k_top)
        bi = jnp.arange(B)[:, None, None]
        hi = jnp.arange(H)[None, :, None]
        mask = jnp.zeros((B, H, L), bool).at[bi, hi, top_idx].set(True)
        q = q * mask[..., None]
        scores = jnp.einsum('bhld,bhmd->bhlm', q, k) * scale
        probs = jax.nn.softmax(scores, axis=-1)
        attn = jnp.einsum('bhlm,bhmd->bhld', probs, v)
        attn = attn.transpose(0, 2, 1, 3).reshape(B, L, D)
        attn_out = attn @ o_w + o_b
        h1 = _layernorm(x + attn_out, ln1_g, ln1_b)
        ff = jax.nn.relu(h1 @ f1_w + f1_b) @ f2_w + f2_b
        h2 = _layernorm(h1 + ff, ln2_g, ln2_b)
        fused = h2 + attn_out
        y = fused.transpose(0, 2, 1)
        y = jax.lax.conv_general_dilated(y, conv_w, window_strides=(1,), padding=[(1, 1)], dimension_numbers=('NCH', 'OIH', 'NCH')) + conv_b[None, :, None]
        y = jax.nn.relu(y)
        y = y.reshape(B, D, L // 2, 2).max(axis=-1)
        return y.transpose(0, 2, 1)

    def _L0_attn_ref(x, norm_w, W_in, conv_w, conv_b, W_dt, b_dt, W_B, W_C, W_out, log_A, D_param, W_ffn1, W_ffn2, W_merge):
        import jax, jax.numpy as jnp
        import numpy as np
        B, T, D, DS, EXP = (1, 512, 128, 32, 2)
        EPS = 1e-06

        def _ssm_scan(xs, dt, Bm, Cm, A):
            log_a = jnp.clip(dt * A[None, None, :], -20.0, 20.0)
            cum = jnp.cumsum(log_a, axis=1)
            dtx = dt * xs
            inp = dtx[..., None] * Bm[:, :, None, :]
            scaled = jnp.exp(-cum)[..., None] * inp
            prefix = jnp.cumsum(scaled, axis=1)
            h_all = jnp.exp(cum)[..., None] * prefix
            return jnp.einsum('btds,bts->btd', h_all, Cm)

        def _forward(x, norm_w, W_in, conv_w, conv_b, W_dt, b_dt, W_B, W_C, W_out, log_A, D_param, W_ffn1, W_ffn2, W_merge):
            r = x
            rms = jnp.sqrt(jnp.mean(x * x, axis=-1, keepdims=True) + EPS)
            xn = x / rms * norm_w
            xz = xn @ W_in
            xs, z = jnp.split(xz, 2, axis=-1)
            xt = jnp.transpose(xs, (0, 2, 1))
            c = jax.lax.conv_general_dilated(xt, conv_w, window_strides=(1,), padding=[(3, 0)], feature_group_count=D, dimension_numbers=('NCH', 'OIH', 'NCH'))
            c = c + conv_b[None, :, None]
            xs = jax.nn.silu(jnp.transpose(c, (0, 2, 1)))
            dt = jax.nn.softplus(xs @ W_dt + b_dt)
            Bm = xs @ W_B
            Cm = xs @ W_C
            A = -jnp.exp(log_A)
            y = _ssm_scan(xs, dt, Bm, Cm, A)
            y_ssm = (y + xs * D_param) * jax.nn.silu(z)
            y_ssm = y_ssm @ W_out
            y_ffn = jax.nn.gelu(xn @ W_ffn1, approximate=False) @ W_ffn2
            y = jnp.concatenate([y_ssm, y_ffn], axis=-1) @ W_merge
            return r + y
        return _forward(x, norm_w, W_in, conv_w, conv_b, W_dt, b_dt, W_B, W_C, W_out, log_A, D_param, W_ffn1, W_ffn2, W_merge)

    def _L0_ffn_ref(x, switch_w, switch_b, expert_w, expert_b):
        import jax, jax.numpy as jnp
        import numpy as np
        CAPACITY_FACTOR = 1.2
        B, S, D = x.shape
        E = switch_w.shape[0]
        N = B * S
        xf = x.reshape(N, D)
        logits = xf @ switch_w.T + switch_b
        probs = jax.nn.softmax(logits, axis=-1)
        route_probs = jnp.max(probs, axis=-1)
        routes = jnp.argmax(probs, axis=-1)
        oh = jax.nn.one_hot(routes, E, dtype=jnp.int32)
        pos = jnp.take_along_axis(jnp.cumsum(oh, axis=0), routes[:, None], axis=1)[:, 0] - 1
        capacity = int(CAPACITY_FACTOR * N / E)
        keep = pos < capacity
        buf = jnp.zeros((E, capacity, D), dtype=xf.dtype).at[routes, pos].set(xf)
        y = jnp.einsum('ecd,efd->ecf', buf, expert_w) + expert_b[:, None, :]
        gathered = y[routes, jnp.minimum(pos, capacity - 1)]
        out = jnp.where(keep[:, None], gathered, xf) * route_probs[:, None]
        return out.reshape(B, S, D)
    h = _L0_tok_ref(x, L0_tok_q_w, L0_tok_q_b, L0_tok_k_w, L0_tok_k_b, L0_tok_v_w, L0_tok_v_b, L0_tok_o_w, L0_tok_o_b, L0_tok_ln1_g, L0_tok_ln1_b, L0_tok_f1_w, L0_tok_f1_b, L0_tok_f2_w, L0_tok_f2_b, L0_tok_ln2_g, L0_tok_ln2_b, L0_tok_conv_w, L0_tok_conv_b)
    h = h + _L0_attn_ref(_layernorm(h, axis=-1), L0_attn_norm_w, L0_attn_W_in, L0_attn_conv_w, L0_attn_conv_b, L0_attn_W_dt, L0_attn_b_dt, L0_attn_W_B, L0_attn_W_C, L0_attn_W_out, L0_attn_log_A, L0_attn_D_param, L0_attn_W_ffn1, L0_attn_W_ffn2, L0_attn_W_merge)
    h = h + _L0_ffn_ref(_layernorm(h, axis=-1), L0_ffn_switch_w, L0_ffn_switch_b, L0_ffn_expert_w, L0_ffn_expert_b)
    return h

_drawn_inputs = setup_inputs


def setup_inputs(seed=0):
    import zlib

    import numpy as np

    out = dict(_drawn_inputs(seed))
    spreads = {'L0_tok_q_b': (0.0, 0.8),
     'L0_tok_k_b': (0.0, 0.8),
     'L0_tok_v_b': (0.0, 0.1),
     'L0_tok_o_b': (0.0, 0.1),
     'L0_tok_ln1_g': (1.0, 0.2),
     'L0_tok_ln1_b': (0.0, 0.1),
     'L0_tok_f1_b': (0.0, 0.1),
     'L0_tok_f2_b': (0.0, 0.1),
     'L0_tok_ln2_g': (1.0, 0.2),
     'L0_tok_ln2_b': (0.0, 0.1),
     'L0_tok_conv_b': (0.0, 0.1),
     'L0_attn_norm_w': (1.0, 0.2),
     'L0_attn_D_param': (1.0, 0.2),
     'L0_ffn_switch_b': (0.0, 0.1),
     'L0_ffn_expert_b': (0.0, 0.8)}
    factors = {'L0_tok_q_w': 8.0,
     'L0_tok_k_w': 8.0,
     'L0_tok_v_w': 8.0,
     'L0_attn_W_dt': 8.0,
     'L0_attn_b_dt': 8.0,
     'L0_attn_W_B': 6.259,
     'L0_attn_W_C': 8.0,
     'L0_attn_log_A': 8.0,
     'L0_ffn_expert_w': 5.031}
    for name, (base, spread) in spreads.items():
        noise = np.random.default_rng([zlib.crc32(name.encode()), seed]).standard_normal(out[name].shape)
        drawn = base * np.exp(spread * noise) if base else spread * noise
        out[name] = jnp.asarray(drawn.astype(out[name].dtype))
    for name, factor in factors.items():
        out[name] = (out[name] * factor).astype(out[name].dtype)
    return out
```

```python
from contextlib import ExitStack

import numpy as np

import concourse.bass as bass
from concourse import mybir

F32 = mybir.dt.float32
BF16 = mybir.dt.bfloat16
ALU = mybir.AluOpType
ACT = mybir.ActivationFunctionType
AX = mybir.AxisListType

B, L, D = 32, 750, 128
H, HD = 8, 16
LC, NL = 125, 6
LH = L // 2
KTOP = int(L * 0.2)
NQ = H * KTOP
QC, NC = 120, 10
PQ = 2 * KTOP
F, NF = 512, 4
T, NT = 375, 3
DS = 32
E = 16
CAP = int(1.2 * B * T / E)
R = B * H
RG = R // 128
BIG = 16.0

VECS = ["q_b", "k_b", "v_b", "o_b", "ln1_g", "ln1_b", "f2_b", "ln2_g", "ln2_b", "conv_b",
        "norm_w", "aconv_b", "b_dt", "log_A", "D_param"]
F1B = len(VECS)
ACW = F1B + NF
NV = ACW + 4


def build(nc, x, w, out):
    ctx = ExitStack()
    with ctx:
        def sb(name, shape, dt=F32):
            return ctx.enter_context(nc.sbuf_tensor(name, shape, dt))

        def sem(name):
            return ctx.enter_context(nc.semaphore(name))

        def dram(name, shape, dt):
            return nc.dram_tensor(name, shape, dt, kind="Internal").ap()

        norms_d = dram("norms_scratch", [R, L], F32)
        place_d = dram("place_scratch", [R, L], BF16)
        h_d = dram("h_scratch", [B, 128, T], F32)

        ps = ctx.enter_context(nc.psum_tensor("ps", [128, 8, 512], F32))

        ident = sb("ident", [128, 128])
        center = sb("center", [128, 128])
        mean = sb("mean", [128, 128])
        headsum = sb("headsum", [128, H])
        kept_iota = sb("kept_iota", [128, KTOP])
        place_of = sb("place_of", [128, NC])
        pair_mask = sb("pair_mask", [128, PQ])
        pair_scale = sb("pair_scale", [128, PQ])
        causal = sb("causal", [LC, T])
        causal16 = sb("causal16", [LC, LC], BF16)
        ones16 = sb("ones16", [LC, LC], BF16)
        tiebreak = sb("tiebreak", [LC, E])

        wq, wk, wv, wo = (sb(n, [128, 128]) for n in ("wq", "wk", "wv", "wo"))
        f1w = sb("f1w", [128, F])
        f2w = sb("f2w", [128, NF, 128])
        cw = sb("cw", [128, 3, 128])
        vec = sb("vec", [128, NV])
        w_in = sb("w_in", [128, 2 * D])
        w_dt = sb("w_dt", [128, D])
        w_b = sb("w_b", [128, DS])
        w_c = sb("w_c", [128, DS])
        ffn1 = sb("ffn1", [128, 2 * D])
        tail = sb("tail", [128, 3, D])
        sw_t = sb("sw_t", [128, E])
        ew_t = sb("ew_t", [128, E * 128])
        eb = sb("eb", [E, 128])
        sb_row = sb("sb_row", [128, E])
        neg_a = sb("neg_a", [128, 1])
        eps5 = sb("eps5", [128, 1])
        eps6 = sb("eps6", [128, 1])
        ones = sb("ones", [128, T])

        place_t = sb("place_t", [LC, NL, R])

        setup = ExitStack()

        def setup_sb(name, shape):
            return setup.enter_context(nc.sbuf_tensor(name, shape, F32))

        cw_raw = setup_sb("cw_raw", [128, 128, 3])
        vec_rows = setup_sb("vec_rows", [NV, 128])
        w_out = setup_sb("w_out", [128, D])
        ffn2 = setup_sb("ffn2", [128, 2, D])
        merge = setup_sb("merge", [128, 2, D])
        out_t = setup_sb("out_t", [128, 3, D])
        sw_rows = setup_sb("sw_rows", [E, 128])
        ew_raw = setup_sb("ew_raw", [128, E, 128])

        def col(name):
            k = VECS.index(name)
            return vec[:, k:k + 1]

        s_w = sem("weights_loaded")
        s_const = sem("constants_made")
        s_turned = sem("weights_turned")
        s_copied = sem("weights_copied")
        n_w = [0]

        with nc.Block() as block:
            @block.sync
            def _(sp):
                def load(dst, src):
                    sp.dma_start(dst, src).then_inc(s_w, 16)
                    n_w[0] += 16
                for k, name in enumerate(VECS):
                    load(vec_rows[k:k + 1, :], w[name].rearrange("(a d) -> a d", a=1))
                load(vec_rows[F1B:F1B + NF, :], w["f1_b"].rearrange("(a d) -> a d", a=NF))
                load(vec[:, ACW:ACW + 4], w["aconv_w"].rearrange("d a k -> d (a k)"))
                for dst, name in ((wq, "q_w"), (wk, "k_w"), (wv, "v_w"), (wo, "o_w"), (f1w, "f1_w"),
                                  (w_in, "W_in"), (w_dt, "W_dt"), (w_b, "W_B"), (w_c, "W_C"),
                                  (w_out, "W_out"), (ffn1, "W_ffn1"), (sw_rows, "switch_w"), (eb, "expert_b")):
                    load(dst[:, :], w[name])
                load(f2w[:, :, :], w["f2_w"].rearrange("(c p) n -> p c n", p=128))
                load(ffn2[:, :, :], w["W_ffn2"].rearrange("(c p) n -> p c n", p=128))
                load(merge[:, :, :], w["W_merge"].rearrange("(c p) n -> p c n", p=128))
                load(cw_raw[:, :, :], w["conv_w"])
                load(ew_raw[:, :, :], w["expert_w"].rearrange("e f d -> f e d"))
                load(sb_row[:, :], w["switch_b"].rearrange("(a e) -> a e", a=1).broadcast_to([128, E]))

            @block.gpsimd
            def _(pool):
                chain = [0]

                def made(ins):
                    ins.then_inc(s_const, 1)
                    chain[0] += 1
                    pool.wait_ge(s_const, chain[0])

                made(pool.memset(ident[:, :], 0.0))
                made(pool.affine_select(out=ident[:, :], in_=ident[:, :], compare_op=ALU.not_equal, fill=1.0,
                                        base=0, pattern=[[-1, 128]], channel_multiplier=1))
                made(pool.memset(mean[:, :], 1.0 / D))
                made(pool.tensor_tensor(center[:, :], ident[:, :], mean[:, :], ALU.subtract))
                made(pool.memset(headsum[:, :], 1.0))
                made(pool.affine_select(out=headsum[:, :], in_=headsum[:, :], compare_op=ALU.is_ge, fill=0.0,
                                        base=0, pattern=[[-HD, H]], channel_multiplier=1))
                made(pool.affine_select(out=headsum[:, :], in_=headsum[:, :], compare_op=ALU.is_ge, fill=0.0,
                                        base=HD - 1, pattern=[[HD, H]], channel_multiplier=-1))
                made(pool.iota(kept_iota[:, :], pattern=[[1, KTOP]], base=1, channel_multiplier=0,
                               allow_small_or_imprecise_dtypes=True))
                made(pool.iota(place_of[:, :], pattern=[[QC, NC]], base=1, channel_multiplier=1,
                               allow_small_or_imprecise_dtypes=True))
                step = pair_scale[:, 0:NC]
                for h in range(1, H):
                    made(pool.memset(step, -float(KTOP)))
                    made(pool.affine_select(out=step, in_=step, compare_op=ALU.is_ge, fill=0.0,
                                            base=-KTOP * h, pattern=[[QC, NC]], channel_multiplier=1))
                    made(pool.tensor_tensor(place_of[:, :], place_of[:, :], step, ALU.add))
                even = pair_mask[:, :].rearrange("p (a k) -> p a k", a=2)
                for i in range(4):
                    half = pair_mask[32 * i:32 * i + 32, :]
                    made(pool.memset(half, 1.0))
                    first, last = half[:, 0:KTOP], half[:, KTOP:PQ]
                    made(pool.affine_select(out=first, in_=first, compare_op=ALU.is_ge, fill=0.0,
                                            base=HD - 1, pattern=[[0, KTOP]], channel_multiplier=-1))
                    made(pool.affine_select(out=last, in_=last, compare_op=ALU.is_ge, fill=0.0,
                                            base=-HD, pattern=[[0, KTOP]], channel_multiplier=1))
                made(pool.tensor_scalar(pair_scale[:, :], pair_mask[:, :], HD ** -0.5, None, ALU.mult))
                made(pool.memset(causal[:, :], 1.0))
                made(pool.affine_select(out=causal[:, :], in_=causal[:, :], compare_op=ALU.is_ge, fill=0.0,
                                        base=0, pattern=[[1, T]], channel_multiplier=-1))
                made(pool.tensor_copy(causal16[:, :], causal[:, 0:LC]))
                made(pool.memset(ones16[:, :], 1.0))
                made(pool.memset(eps5[:, :], 1e-5))
                made(pool.memset(eps6[:, :], 1e-6))
                made(pool.memset(ones[:, :], 1.0))
                made(pool.iota(tiebreak[:, :], pattern=[[-1, E]], base=E, channel_multiplier=0,
                               allow_small_or_imprecise_dtypes=True))
                assert chain[0] == N_CONST, chain[0]

            @block.tensor
            def _(pe):
                pe.wait_ge(s_const, N_CONST)
                pe.wait_ge(s_w, n_w[0])
                pe.transpose(ps[:, 0, 0:ACW], vec_rows[0:ACW, :], ident[0:ACW, 0:ACW])
                for k in range(3):
                    pe.transpose(ps[:, 1, 128 * k:128 * k + 128], cw_raw[:, :, k], ident[:, :])
                pe.transpose(ps[:, 2, 0:128], w_out[:, :], ident[:, :])
                for k in range(2):
                    pe.transpose(ps[:, 2, 128 * k + 128:128 * k + 256], ffn2[:, k, :], ident[:, :])
                pe.transpose(ps[:, 3, 0:E], sw_rows[:, :], ident[0:E, 0:E])
                for e in range(E):
                    last = pe.transpose(ps[:, 4 + e // 4, 128 * (e % 4):128 * (e % 4) + 128], ew_raw[:, e, :],
                                        ident[:, :])
                last.then_inc(s_turned, 1)
                pe.wait_ge(s_copied, 4)
                for k in range(3):
                    last = pe.matmul(ps[:, 0, 128 * k:128 * k + 128], out_t[:, k, :],
                                     merge[:, 0 if k == 0 else 1, :], start=True, stop=True)
                last.then_inc(s_turned, 1)

            @block.vector
            def _(dve):
                dve.wait_ge(s_turned, 1)
                dve.tensor_copy(vec[:, 0:ACW], ps[:, 0, 0:ACW]).then_inc(s_copied, 1)
                dve.tensor_copy(cw[:, :, :], ps[:, 1, 0:384].rearrange("p (k n) -> p k n", k=3)).then_inc(s_copied, 1)
                dve.tensor_copy(out_t[:, :, :], ps[:, 2, 0:384].rearrange("p (k n) -> p k n", k=3))\
                   .then_inc(s_copied, 1)
                dve.tensor_copy(sw_t[:, :], ps[:, 3, 0:E]).then_inc(s_copied, 1)
                for k in range(4):
                    dve.tensor_copy(ew_t[:, 512 * k:512 * k + 512], ps[:, 4 + k, :]).then_inc(s_copied, 1)
                dve.wait_ge(s_turned, 2)
                dve.tensor_copy(tail[:, :, :], ps[:, 0, 0:384].rearrange("p (k n) -> p k n", k=3))\
                   .then_inc(s_copied, 1)

            @block.scalar
            def _(act):
                act.wait_ge(s_copied, 1)
                act.activation(neg_a[:, :], col("log_A"), ACT.Exp).then_inc(s_a := sem("a_exp"), 1)
                act.wait_ge(s_a, 1)
                act.mul(neg_a[:, :], neg_a[:, :], -1.0).then_inc(s_a, 1)
                act.wait_ge(s_a, 2)

        setup.close()

        with ExitStack() as part, nc.Block() as block:
            xin = part.enter_context(nc.sbuf_tensor("a_xin", [LC, 2, NL, 128], F32))
            xt = part.enter_context(nc.sbuf_tensor("a_xt", [128, 2, 2, LH], F32))
            sq = part.enter_context(nc.sbuf_tensor("a_sq", [128, 2, 2, LH], F32))
            nrm = part.enter_context(nc.sbuf_tensor("a_nrm", [H, 2, 2, LH], F32))
            s_in = [sem(f"a_x_loaded{k}") for k in range(2)]
            s_xt = sem("a_x_turned")
            s_xc = sem("a_xt_ready")
            s_q = sem("a_q_done")
            s_sq = sem("a_squares_ready")
            s_n = sem("a_norms_done")
            s_nc = sem("a_norms_ready")
            s_no = [sem(f"a_norms_stored{k}") for k in range(2)]

            @block.sync
            def _(sp):
                for one in (s_xc, s_sq, s_nc):
                    sp.sem_inc(one, 1)
                for k in range(2):
                    sp.sem_inc(s_no[k], 16)
                for k in range(2):
                    sp.dma_start(xin[:, k], x[k].rearrange("(c p) d -> p c d", p=LC)).then_inc(s_in[k], 16)

                def store(i, k):
                    sp.wait_ge(s_nc, 2 * i + k + 2)
                    sp.dma_start(norms_d[bass.ds(H * (2 * i + k), H), :].rearrange("h (n l) -> h n l", n=2),
                                 nrm[:, k]).then_inc(s_no[k], 16)

                with sp.Fori(0, B // 2 - 1) as i:
                    for k in range(2):
                        sp.wait_ge(s_xt, 2 * i + k + 1)
                        sp.dma_start(xin[:, k], x[bass.ds(2 * i + k + 2, 1)].rearrange("a (c p) d -> p (a c) d", p=LC))\
                          .then_inc(s_in[k], 16)
                        store(i, k)
                for k in range(2):
                    store(B // 2 - 1, k)
                for k in range(2):
                    sp.wait_ge(s_no[k], 16 * (B // 2) + 16)

            @block.tensor
            def _(pe):
                with pe.Fori(0, B // 2) as i:
                    for k in range(2):
                        pe.wait_ge(s_in[k], 16 * i + 16)
                        pe.wait_ge(s_xc, 2 * i + k + 1)
                        for c in range(NL):
                            last = pe.transpose(ps[:, c // 3, LC * (c % 3):LC * (c % 3) + LC], xin[:, k, c, :],
                                                ident[0:LC, 0:LC])
                        last.then_inc(s_xt, 1)
                        pe.wait_ge(s_xc, 2 * i + k + 1 + 1)
                        pe.wait_ge(s_sq, 2 * i + k + 1)
                        for n in range(2):
                            last = pe.matmul(ps[:, 2 + n, 0:LH], wq[:, :], xt[:, k, n, :], start=True, stop=True)
                        last.then_inc(s_q, 1)
                        pe.wait_ge(s_sq, 2 * i + k + 1 + 1)
                        pe.wait_ge(s_nc, 2 * i + k + 1)
                        for n in range(2):
                            last = pe.matmul(ps[0:H, 4 + n, 0:LH], headsum[:, :], sq[:, k, n, :], start=True, stop=True)
                        last.then_inc(s_n, 1)

            @block.scalar
            def _(act):
                with act.Fori(0, B // 2) as i:
                    for k in range(2):
                        act.wait_ge(s_q, 2 * i + k + 1)
                        act.activation(sq[:, k], ps[:, 2:4, 0:LH], ACT.Square, bias=col("q_b")).then_inc(s_sq, 1)

            @block.vector
            def _(dve):
                with dve.Fori(0, B // 2) as i:
                    for k in range(2):
                        dve.wait_ge(s_xt, 2 * i + k + 1)
                        dve.tensor_copy(xt[:, k], ps[:, 0:2, 0:LH]).then_inc(s_xc, 1)
                        dve.wait_ge(s_n, 2 * i + k + 1)
                        dve.wait_ge(s_no[k], 16 * i + 16)
                        dve.tensor_copy(nrm[:, k], ps[0:H, 4:6, 0:LH]).then_inc(s_nc, 1)

        with ExitStack() as part, nc.Block() as block:
            work = part.enter_context(nc.sbuf_tensor("k_work", [128, RG, L], F32))
            mask = part.enter_context(nc.sbuf_tensor("k_mask", [128, RG, L], F32))
            count = part.enter_context(nc.sbuf_tensor("k_count", [128, RG, L], F32))
            place = part.enter_context(nc.sbuf_tensor("k_place", [128, RG, L], F32))
            place16 = part.enter_context(nc.sbuf_tensor("k_place16", [128, RG, L], BF16))
            top8 = part.enter_context(nc.sbuf_tensor("k_top8", [128, RG, 8], F32))
            s_l = sem("k_norms_loaded")
            s_m = [sem(f"k_max_found{g}") for g in range(RG)]
            s_r = [sem(f"k_max_removed{g}") for g in range(RG)]
            s_k = sem("k_step")
            s_seen = sem("k_wait_seen")
            s_t = sem("k_places_turned")
            s_tc = sem("k_places_copied")
            s_p16 = sem("k_places16_ready")
            s_ps = sem("k_places_stored")
            FULL = KTOP // 8

            @block.sync
            def _(sp):
                for g in range(RG):
                    sp.sem_inc(s_r[g], 1)
                sp.dma_start(work[:, :, :], norms_d.rearrange("(g p) l -> p g l", p=128)).then_inc(s_l, 16)
                sp.wait_ge(s_p16, RG)
                sp.dma_start(place_d.rearrange("(g p) l -> p g l", p=128), place16[:, :, :]).then_inc(s_ps, 16)
                sp.wait_ge(s_ps, 16)

            @block.vector
            def _(dve):
                dve.wait_ge(s_l, 16)
                with dve.Fori(0, FULL) as i:
                    for g in range(RG):
                        dve.wait_ge(s_r[g], i + 1)
                        dve.sem_inc(s_seen, 1)
                        dve.max(top8[:, g, :], work[:, g, :]).then_inc(s_m[g], 1)
                    for g in range(RG):
                        dve.wait_ge(s_m[g], i + 1)
                        dve.sem_inc(s_seen, 1)
                        dve.match_replace(work[:, g, :], top8[:, g, :], work[:, g, :], -1.0).then_inc(s_r[g], 1)
                for g in range(RG):
                    dve.wait_ge(s_r[g], FULL + 1)
                    dve.max(top8[:, g, :], work[:, g, :]).then_inc(s_m[g], 1)
                for g in range(RG):
                    dve.wait_ge(s_m[g], FULL + 1)
                    dve.memset(top8[:, g, KTOP % 8:8], -1.0).then_inc(s_m[g], 1)
                for g in range(RG):
                    dve.wait_ge(s_m[g], FULL + 2)
                    dve.match_replace(work[:, g, :], top8[:, g, :], work[:, g, :], -1.0).then_inc(s_r[g], 1)
                n = 0
                for g in range(RG):
                    dve.wait_ge(s_r[g], FULL + 1 + 1)
                    dve.tensor_scalar(mask[:, g, :], work[:, g, :], 0.0, None, ALU.is_lt).then_inc(s_k, 1)
                    n += 1
                for g in range(RG):
                    dve.wait_ge(s_k, g + 1)
                    dve.tensor_tensor_scan(count[:, g, :], mask[:, g, :], mask[:, g, :], 0.0, ALU.add, ALU.max)\
                       .then_inc(s_k, 1)
                for g in range(RG):
                    dve.wait_ge(s_k, RG + g + 1)
                    dve.tensor_tensor(place[:, g, :], count[:, g, :], mask[:, g, :], ALU.mult).then_inc(s_k, 1)
                for g in range(RG):
                    dve.wait_ge(s_k, 2 * RG + g + 1)
                    dve.tensor_copy(place16[:, g, :], place[:, g, :]).then_inc(s_p16, 1)
                for c in range(NL):
                    dve.wait_ge(s_t, c + 1)
                    dve.tensor_copy(place_t[:, c, :], ps[0:LC, c, 0:R]).then_inc(s_tc, 1)

            @block.tensor
            def _(pe):
                pe.wait_ge(s_k, 3 * RG)
                for c in range(NL):
                    for g in range(RG):
                        last = pe.transpose(ps[0:LC, c, 128 * g:128 * g + 128], place[:, g, LC * c:LC * c + LC],
                                            ident[:, :])
                    last.then_inc(s_t, 1)

        with ExitStack() as part:
            attention_part(nc, part, locals())

        with ExitStack() as part:
            expert_part(nc, part, locals())


N_CONST = 8 + 1 + 3 * (H - 1) + 4 * 3 + 1 + 2 + 6


class Chain:

    def __init__(self, eng, step_done, i, per_turn):
        self.eng, self.step_done, self.base, self.n, self.per = eng, step_done, i * per_turn, 0, per_turn

    def __call__(self, ins):
        ins.then_inc(self.step_done, 1)
        self.n += 1
        self.eng.wait_ge(self.step_done, self.base + self.n)

    def end(self):
        assert self.n == self.per, self.n


def attention_part(nc, part, v):
    ps, ident, center, mean, vec = v["ps"], v["ident"], v["center"], v["mean"], v["vec"]
    wq, wk, wv, wo, f1w, f2w, cw = (v[n] for n in ("wq", "wk", "wv", "wo", "f1w", "f2w", "cw"))
    pair_mask, pair_scale, kept_iota, place_of = (v[n] for n in ("pair_mask", "pair_scale", "kept_iota", "place_of"))
    place_t, place_d, h_d, x, col, sem = (v[n] for n in ("place_t", "place_d", "h_d", "x", "col", "sem"))

    def sb(name, shape, dt=F32):
        return part.enter_context(nc.sbuf_tensor(name, shape, dt))

    xin = sb("c_xin", [LC, NL, 128])
    xt = sb("c_xt", [128, 2, LH])
    xc = sb("c_xc", [128, 2, LH])
    xmean = sb("c_xmean", [128, 1])
    mv = sb("c_mv", [128, 1])
    mo = sb("c_mo", [128, 1])
    kt = sb("c_kt", [128, 2, LH])
    qtok = sb("c_qtok", [LC, NL, 128])
    vtok = sb("c_vtok", [LC, NL, 128])
    pick = sb("c_pick", [LC, NL, NQ])
    place = sb("c_place", [LC, NL, H])
    spread = sb("c_spread", [QC, NC, L], BF16)
    place_b = sb("c_place_b", [QC, NC, L], BF16)
    blk = sb("c_blk", [128, NQ])
    ablk = sb("c_ablk", [128, NQ])
    prob = sb("c_prob", [QC, 2, L])
    probt = sb("c_probt", [LC, NL, NQ])
    nmax = sb("c_nmax", [QC, NC])
    den = sb("c_den", [QC, NC])
    rden = sb("c_rden", [QC, NC])
    z = sb("c_z", [QC, NC, 128])
    zres = sb("c_zres", [QC, NC, 128])
    zpart = [sb(f"c_zpart{k}", [QC, NC, 128], BF16) for k in range(3)]
    ao = sb("c_ao", [128, 2, LH])
    hid = sb("c_hid", [128, 2, LH])
    sq = sb("c_sq", [128, 2, LH])
    rstd = sb("c_rstd", [128, 2, LH])
    ff = sb("c_ff", [128, NF, 2, LH])
    fused = sb("c_fused", [128, L + 2])
    pooled = sb("c_pooled", [128, T])
    hout = sb("c_hout", [128, T])

    names = """x_loaded x_turned xt_ready mean_ready k_done q_done v_done mv_done kt_ready q_ready v_ready
        mv_ready mo_done mo_ready place_ready pick_ready gathered blk_ready scored max_ready prob_ready
        prob_turned probt_dve probt_act av_done ablk_ready z_done z_part0 z_part1 z_res z_part2 place_loaded
        spread_ready spread_done ao_ready res_ready centered squared var_done rstd_ready normed f1_done ff_act
        ff_dve f2_done fused_ready conv_done pooled_ready h_ready dve_step act_step zeroed h_stored pool_seen""".split()
    s = {n: sem("c_" + n) for n in names}
    runs = []
    for c in range(NC // 2):
        q = QC * c
        while q < QC * (c + 1):
            h = q // KTOP
            n = min(KTOP * (h + 1), QC * (c + 1)) - q
            runs.append((c, q - QC * c, n, h))
            q += n

    with nc.Block() as block:
        @block.sync
        def _(sp):
            for n in ("x_turned", "gathered", "h_ready", "pick_ready", "spread_ready"):
                sp.sem_inc(s[n], 1)
            sp.sem_inc(s["h_stored"], 16)
            with sp.Fori(0, B) as i:
                sp.wait_ge(s["x_turned"], i + 1)
                sp.dma_start(xin[:, :, :], x[bass.ds(i, 1)].rearrange("a (c p) d -> p (a c) d", p=LC))\
                  .then_inc(s["x_loaded"], 16)
                sp.wait_ge(s["spread_ready"], NC * i + 1)
                for c, p, n, h in runs:
                    src = place_d[bass.ds(H * i, H), :].rearrange("(a h) l -> h a l", a=2)[h:h + 1]
                    sp.dma_start(place_b[p:p + n, c::NC // 2, :], src.broadcast_to([n, 2, L]))\
                      .then_inc(s["place_loaded"], 16)

        @block.gpsimd
        def _(pool):
            pool.memset(blk[:, :], 0.0).then_inc(s["zeroed"], 1)
            pool.memset(ablk[:, :], 0.0).then_inc(s["zeroed"], 1)
            pool.memset(fused[:, :], 0.0).then_inc(s["zeroed"], 1)
            with pool.Fori(0, B) as i:
                pool.wait_ge(s["place_ready"], i + 1)
                pool.wait_ge(s["gathered"], i + 1)
                pool.sem_inc(s["pool_seen"], 1)
                for c in range(NL):
                    for h in range(H):
                        last = pool.tensor_scalar(pick[:, c, KTOP * h:KTOP * h + KTOP], kept_iota[0:LC, :],
                                                  place[:, c, h:h + 1], None, ALU.is_equal)
                    last.then_inc(s["pick_ready"], 1)

        @block.scalar
        def _(act):
            act.preload_act_table_set("natural_log_exp_and_others")
            act.wait_ge(s["zeroed"], 3)
            with act.Fori(0, B) as i:
                step = Chain(act, s["act_step"], i, 2)
                act.wait_ge(s["x_turned"], i + 1 + 1)
                act.activation(xt[:, :, :], ps[:, 0:2, 0:LH], ACT.Copy).then_inc(s["xt_ready"], 1)
                act.wait_ge(s["k_done"], i + 1)
                act.activation(kt[:, :, :], ps[:, 2:4, 0:LH], ACT.Identity, bias=col("k_b")).then_inc(s["kt_ready"], 1)
                act.wait_ge(s["q_done"], i + 1)
                act.activation(qtok[:, :, :].rearrange("p (b c) d -> p b (c d)", b=2), ps[0:LC, 4:6, 0:384],
                               ACT.Copy).then_inc(s["q_ready"], 1)

                def exp_chunk(c):
                    act.wait_ge(s["max_ready"], NC * i + c + 1)
                    if c >= 2:
                        act.wait_ge(s["prob_turned"], NC * i + c - 1)
                    a = 2 + 2 * (c % 2)
                    act.activation(prob[:, c % 2, :].rearrange("p (n l) -> p n l", n=2), ps[0:QC, a:a + 2, 0:LH],
                                   ACT.Exp, bias=nmax[:, c:c + 1], accum_out=den[:, c:c + 1])\
                       .then_inc(s["prob_ready"], 1)

                def copy_chunk(c):
                    act.wait_ge(s["prob_turned"], NC * i + c + 1)
                    act.activation(probt[:, 3:6, QC * c:QC * c + QC],
                                   ps[0:LC, 7, 0:3 * QC].rearrange("p (c q) -> p c q", c=3), ACT.Copy)\
                       .then_inc(s["probt_act"], 1)

                exp_chunk(0)
                for c in range(1, NC):
                    exp_chunk(c)
                    copy_chunk(c - 1)
                copy_chunk(NC - 1)
                act.wait_ge(s["z_part0"], i + 1)
                act.activation(zpart[0][:, :, :], z[:, :, :], ACT.Copy).then_inc(s["z_part1"], 1)
                act.wait_ge(s["z_res"], i + 1)
                act.activation(zpart[1][:, :, :], zres[:, :, :], ACT.Copy).then_inc(s["z_part1"], 1)
                act.wait_ge(s["spread_done"], i + 1)
                act.wait_ge(s["mo_ready"], i + 1)
                act.activation(ao[:, :, :], ps[:, 6:8, 0:LH], ACT.Identity, bias=mo[:, 0:1]).then_inc(s["ao_ready"], 1)

                def layer_norm(n):
                    act.wait_ge(s["centered"], 2 * i + n + 1)
                    act.activation(sq[:, :, :], ps[:, 0:2, 0:LH], ACT.Square).then_inc(s["squared"], 1)
                    act.wait_ge(s["var_done"], 2 * i + n + 1)
                    step(act.activation(rstd[:, :, :], ps[:, 2:4, 0:LH], ACT.Ln, bias=v["eps5"][:, 0:1]))
                    act.activation(rstd[:, :, :], rstd[:, :, :], ACT.Exp, scale=-0.5).then_inc(s["rstd_ready"], 1)

                layer_norm(0)
                for k in (0, 2):
                    act.wait_ge(s["f1_done"], NF * i + k + 1)
                    act.activation(ff[:, k], ps[:, 2:4, 0:LH], ACT.Relu, bias=vec[:, F1B + k:F1B + k + 1])\
                       .then_inc(s["ff_act"], 1)
                layer_norm(1)
                act.wait_ge(s["pooled_ready"], i + 1)
                act.wait_ge(s["h_stored"], 16 * i + 16)
                act.activation(hout[:, :], pooled[:, :], ACT.Relu, bias=col("conv_b")).then_inc(s["h_ready"], 1)
                act.wait_ge(s["h_ready"], i + 2)
                act.dma_start(h_d[bass.ds(i, 1)].rearrange("a p t -> p (a t)"), hout[:, :])\
                   .then_inc(s["h_stored"], 16)
                step.end()
            act.wait_ge(s["h_stored"], 16 * B + 16)

        @block.tensor
        def _(pe):
            pe.wait_ge(s["zeroed"], 3)
            with pe.Fori(0, B) as i:
                pe.wait_ge(s["x_loaded"], 16 * i + 16)
                pe.wait_ge(s["h_ready"], i + 1)
                for c in range(NL):
                    last = pe.transpose(ps[:, c // 3, LC * (c % 3):LC * (c % 3) + LC], xin[:, c, :],
                                        ident[0:LC, 0:LC])
                last.then_inc(s["x_turned"], 1)
                pe.wait_ge(s["xt_ready"], i + 1)
                flat = xt[:, :, :].rearrange("p n l -> p (n l)")
                for n in range(2):
                    last = pe.matmul(ps[:, 2 + n, 0:LH], wk[:, :], xt[:, n, :], start=True, stop=True)
                last.then_inc(s["k_done"], 1)
                for c in range(NL):
                    last = pe.matmul(ps[0:LC, 4 + c // 3, 128 * (c % 3):128 * (c % 3) + 128],
                                     flat[:, LC * c:LC * c + LC], wq[:, :], start=True, stop=True)
                last.then_inc(s["q_done"], 1)
                pe.wait_ge(s["mean_ready"], i + 1)
                flat = xc[:, :, :].rearrange("p n l -> p (n l)")
                for c in range(NL):
                    last = pe.matmul(ps[0:LC, 6 + c // 3, 128 * (c % 3):128 * (c % 3) + 128],
                                     flat[:, LC * c:LC * c + LC], wv[:, :], start=True, stop=True)
                last.then_inc(s["v_done"], 1)
                pe.matmul(ps[:, 0, 0:1], wv[:, :], xmean[:, 0:1], start=True, stop=True).then_inc(s["mv_done"], 1)
                pe.wait_ge(s["mv_ready"], i + 1)
                pe.matmul(ps[:, 1, 0:1], wo[:, :], mv[:, 0:1], start=True, stop=True).then_inc(s["mo_done"], 1)

                pe.wait_ge(s["q_ready"], i + 1)
                for c in range(NL):
                    pe.wait_ge(s["pick_ready"], NL * i + c + 1 + 1)
                    for j in range(4):
                        last = pe.matmul(ps[32 * j:32 * j + 32, 0, 0:PQ], qtok[:, c, 32 * j:32 * j + 32],
                                         pick[:, c, PQ * j:PQ * j + PQ], start=(c == 0), stop=(c == NL - 1),
                                         skip_group_check=True)
                last.then_inc(s["gathered"], 1)

                pe.wait_ge(s["blk_ready"], i + 1)
                pe.wait_ge(s["kt_ready"], i + 1)

                def scores(c):
                    if c >= 2:
                        pe.wait_ge(s["prob_ready"], NC * i + c - 1)
                    for n in range(2):
                        last = pe.matmul(ps[0:QC, 2 + 2 * (c % 2) + n, 0:LH], blk[:, QC * c:QC * c + QC],
                                         kt[:, n, :], start=True, stop=True)
                    last.then_inc(s["scored"], 1)

                def turn(c):
                    pe.wait_ge(s["prob_ready"], NC * i + c + 1)
                    if c == 0:
                        pe.wait_ge(s["v_ready"], i + 1)
                    else:
                        pe.wait_ge(s["probt_dve"], NC * i + c)
                        pe.wait_ge(s["probt_act"], NC * i + c)
                    for m in range(NL):
                        last = pe.transpose(ps[0:LC, 6 + m // 3, QC * (m % 3):QC * (m % 3) + QC],
                                            prob[:, c % 2, LC * m:LC * m + LC], ident[0:QC, 0:QC])
                    last.then_inc(s["prob_turned"], 1)

                scores(0)
                for c in range(1, NC):
                    scores(c)
                    turn(c - 1)
                turn(NC - 1)
                pe.wait_ge(s["probt_dve"], NC * i + NC)
                pe.wait_ge(s["probt_act"], NC * i + NC)
                for c in range(NL):
                    for j in range(4):
                        last = pe.matmul(ps[32 * j:32 * j + 32, 0, 0:PQ], vtok[:, c, 32 * j:32 * j + 32],
                                         probt[:, c, PQ * j:PQ * j + PQ], start=(c == 0), stop=(c == NL - 1),
                                         skip_group_check=True)
                last.then_inc(s["av_done"], 1)
                pe.wait_ge(s["ablk_ready"], i + 1)
                for c in range(NC):
                    last = pe.matmul(ps[0:QC, 2 + c // 4, 128 * (c % 4):128 * (c % 4) + 128],
                                     ablk[:, QC * c:QC * c + QC], wo[:, :], start=True, stop=True)
                last.then_inc(s["z_done"], 1)
                pe.wait_ge(s["spread_ready"], NC * i + NC + 1)
                pe.wait_ge(s["z_part1"], 2 * i + 2)
                pe.wait_ge(s["z_part2"], i + 1)
                for n in range(2):
                    for k in range(3):
                        for c in range(NC):
                            last = pe.matmul(ps[:, 6 + n, 0:LH], zpart[k][:, c, :], spread[:, c, LH * n:LH * n + LH],
                                             start=(k == 0 and c == 0), stop=(k == 2 and c == NC - 1))
                last.then_inc(s["spread_done"], 1)

                def layer_norm(n):
                    pe.wait_ge(s["res_ready"], 2 * i + n + 1)
                    for m in range(2):
                        last = pe.matmul(ps[:, m, 0:LH], center[:, :], xc[:, m, :], start=True, stop=True)
                    last.then_inc(s["centered"], 1)
                    pe.wait_ge(s["squared"], 2 * i + n + 1)
                    for m in range(2):
                        last = pe.matmul(ps[:, 2 + m, 0:LH], mean[:, :], sq[:, m, :], start=True, stop=True)
                    last.then_inc(s["var_done"], 1)

                layer_norm(0)
                pe.wait_ge(s["normed"], 2 * i + 1)
                for k in range(NF):
                    if k == 2:
                        pe.wait_ge(s["ff_act"], 2 * i + 1)
                    if k == 3:
                        pe.wait_ge(s["ff_dve"], 2 * i + 1)
                    for n in range(2):
                        last = pe.matmul(ps[:, 2 + 2 * (k % 2) + n, 0:LH], f1w[:, 128 * k:128 * k + 128],
                                         hid[:, n, :], start=True, stop=True)
                    last.then_inc(s["f1_done"], 1)
                for k in range(NF):
                    pe.wait_ge(s["ff_dve" if k % 2 else "ff_act"], 2 * i + k // 2 + 1)
                    for n in range(2):
                        last = pe.matmul(ps[:, 6 + n, 0:LH], f2w[:, k, :], ff[:, k, n, :],
                                         start=(k == 0), stop=(k == NF - 1))
                last.then_inc(s["f2_done"], 1)
                layer_norm(1)
                pe.wait_ge(s["fused_ready"], i + 1)
                for n, (a, m) in enumerate(((0, LH + 1), (LH + 1, LH - 1))):
                    for k in range(3):
                        last = pe.matmul(ps[:, 4 + n, 0:m], cw[:, k, :], fused[:, a + k:a + k + m],
                                         start=(k == 0), stop=(k == 2))
                last.then_inc(s["conv_done"], 1)

        @block.vector
        def _(dve):
            dve.wait_ge(s["zeroed"], 3)
            with dve.Fori(0, B) as i:
                step = Chain(dve, s["dve_step"], i, 6)
                dve.wait_ge(s["pick_ready"], NL * i + 1)
                dve.tensor_copy(place[:, :, :], place_t[:, :, bass.ds(H * i, H)]).then_inc(s["place_ready"], 1)
                dve.wait_ge(s["xt_ready"], i + 1)
                step(dve.tensor_reduce(xmean[:, :], xt[:, :, :], AX.XY, ALU.add))
                step(dve.tensor_scalar(xmean[:, :], xmean[:, :], 1.0 / L, None, ALU.mult))
                dve.tensor_scalar(xc[:, :, :], xt[:, :, :], xmean[:, 0:1], None, ALU.subtract)\
                   .then_inc(s["mean_ready"], 1)
                dve.wait_ge(s["v_done"], i + 1)
                dve.tensor_copy(vtok[:, :, :].rearrange("p (b c) d -> p b (c d)", b=2), ps[0:LC, 6:8, 0:384])\
                   .then_inc(s["v_ready"], 1)
                dve.wait_ge(s["mv_done"], i + 1)
                dve.tensor_scalar(mv[:, :], ps[:, 0, 0:1], col("v_b"), None, ALU.add).then_inc(s["mv_ready"], 1)
                dve.wait_ge(s["mo_done"], i + 1)
                dve.tensor_scalar(mo[:, :], ps[:, 1, 0:1], col("o_b"), None, ALU.add).then_inc(s["mo_ready"], 1)
                dve.wait_ge(s["gathered"], i + 1 + 1)
                for j in range(4):
                    p = slice(32 * j, 32 * j + 32)
                    last = dve.scalar_tensor_tensor(out=blk[p, PQ * j:PQ * j + PQ], in0=ps[p, 0, 0:PQ],
                                                    scalar=col("q_b")[p], in1=pair_scale[p, :],
                                                    op0=ALU.add, op1=ALU.mult)
                last.then_inc(s["blk_ready"], 1)

                def row_max(c):
                    dve.wait_ge(s["scored"], NC * i + c + 1)
                    a = 2 + 2 * (c % 2)
                    dve.tensor_reduce(nmax[:, c:c + 1], ps[0:QC, a:a + 2, 0:LH], AX.XY, ALU.max, negate=True)\
                       .then_inc(s["max_ready"], 1)

                def copy_chunk(c):
                    dve.wait_ge(s["prob_turned"], NC * i + c + 1)
                    dve.tensor_copy(probt[:, 0:3, QC * c:QC * c + QC],
                                    ps[0:LC, 6, 0:3 * QC].rearrange("p (c q) -> p c q", c=3))\
                       .then_inc(s["probt_dve"], 1)

                row_max(0)
                dve.wait_ge(s["place_loaded"], 16 * len(runs) * i + 16 * len(runs))
                for c in range(NC):
                    if c + 1 < NC:
                        row_max(c + 1)
                    dve.tensor_scalar(spread[:, c, :], place_b[:, c, :], place_of[0:QC, c:c + 1], None,
                                      ALU.is_equal).then_inc(s["spread_ready"], 1)
                    copy_chunk(c)
                dve.wait_ge(s["prob_ready"], NC * i + NC)
                step(dve.reciprocal(rden[:, :], den[:, :]))
                dve.wait_ge(s["av_done"], i + 1)
                for j in range(4):
                    p = slice(32 * j, 32 * j + 32)
                    last = dve.tensor_tensor(ablk[p, PQ * j:PQ * j + PQ], ps[p, 0, 0:PQ], pair_mask[p, :], ALU.mult)
                last.then_inc(s["ablk_ready"], 1)
                dve.wait_ge(s["z_done"], i + 1)
                zps = ps[0:QC, 2:5, :].rearrange("p b n -> p (b n)")[:, 0:NC * 128].rearrange("p (c n) -> p c n", c=NC)
                dve.tensor_tensor(z[:, :, :], zps, rden[:, :, None].broadcast_to([QC, NC, 128]), ALU.mult)\
                   .then_inc(s["z_part0"], 1)
                dve.wait_ge(s["z_part1"], 2 * i + 1)
                dve.tensor_tensor(zres[:, :, :], z[:, :, :], zpart[0][:, :, :], ALU.subtract).then_inc(s["z_res"], 1)
                dve.wait_ge(s["z_part1"], 2 * i + 2)
                dve.tensor_tensor(zpart[2][:, :, :], zres[:, :, :], zpart[1][:, :, :], ALU.subtract)\
                   .then_inc(s["z_part2"], 1)
                dve.wait_ge(s["ao_ready"], i + 1)
                dve.tensor_tensor(xc[:, :, :], xt[:, :, :], ao[:, :, :], ALU.add).then_inc(s["res_ready"], 1)

                def layer_norm(n, g, b):
                    dve.wait_ge(s["rstd_ready"], 2 * i + n + 1)
                    step(dve.tensor_tensor(hid[:, :, :], ps[:, 0:2, 0:LH], rstd[:, :, :], ALU.mult))
                    return dve.tensor_scalar(hid[:, :, :], hid[:, :, :], col(g), col(b), ALU.mult, ALU.add)

                layer_norm(0, "ln1_g", "ln1_b").then_inc(s["normed"], 1)
                for k in (1, 3):
                    dve.wait_ge(s["f1_done"], NF * i + k + 1)
                    dve.tensor_scalar(ff[:, k], ps[:, 4:6, 0:LH], vec[:, F1B + k:F1B + k + 1], 0.0,
                                      ALU.add, ALU.max).then_inc(s["ff_dve"], 1)
                dve.wait_ge(s["f2_done"], i + 1)
                dve.wait_ge(s["normed"], 2 * i + 1)
                dve.scalar_tensor_tensor(out=xc[:, :, :], in0=ps[:, 6:8, 0:LH], scalar=col("f2_b"), in1=hid[:, :, :],
                                         op0=ALU.add, op1=ALU.add).then_inc(s["res_ready"], 1)
                layer_norm(1, "ln2_g", "ln2_b").then_inc(s["normed"], 1)
                dve.wait_ge(s["normed"], 2 * i + 2)
                dve.tensor_tensor(fused[:, 1:L + 1].rearrange("p (n l) -> p n l", n=2), hid[:, :, :], ao[:, :, :],
                                  ALU.add).then_inc(s["fused_ready"], 1)
                dve.wait_ge(s["conv_done"], i + 1)
                m = (LH + 1) // 2
                step(dve.tensor_reduce(pooled[:, 0:m], ps[:, 4, 0:2 * m].rearrange("p (t two) -> p t two", two=2),
                                       AX.X, ALU.max))
                dve.tensor_reduce(pooled[:, m:T], ps[:, 5, 0:2 * (T - m)].rearrange("p (t two) -> p t two", two=2),
                                  AX.X, ALU.max).then_inc(s["pooled_ready"], 1)
                step.end()


def expert_part(nc, part, v):
    ps, ident, center, mean, vec = v["ps"], v["ident"], v["center"], v["mean"], v["vec"]
    w_in, w_dt, w_b, w_c, ffn1, tail = (v[n] for n in ("w_in", "w_dt", "w_b", "w_c", "ffn1", "tail"))
    sw_t, ew_t, eb, sb_row, neg_a = (v[n] for n in ("sw_t", "ew_t", "eb", "sb_row", "neg_a"))
    causal, causal16, ones16, tiebreak = (v[n] for n in ("causal", "causal16", "ones16", "tiebreak"))
    h_d, out, col, sem = (v[n] for n in ("h_d", "out", "col", "sem"))

    def sb(name, shape, dt=F32):
        return part.enter_context(nc.sbuf_tensor(name, shape, dt))

    hin = sb("e_hin", [128, T])
    hb = sb("e_hb", [128, T])
    sq = sb("e_sq", [128, T])
    rstd = sb("e_rstd", [128, T])
    u = sb("e_u", [128, T])
    xn = sb("e_xn", [128, T])
    xp = sb("e_xp", [128, T + 3])
    c = sb("e_c", [128, T])
    th = sb("e_th", [128, 2, T])
    g = sb("e_g", [128, 2, T])
    xs = sb("e_xs", [128, T])
    sz = sb("e_sz", [128, T])
    ee = sb("e_ee", [128, T])
    w1 = sb("e_w1", [128, T])
    lw = sb("e_lw", [128, T])
    t1 = sb("e_t1", [128, T])
    t2 = sb("e_t2", [128, T])
    dt = sb("e_dt", [128, T])
    la = sb("e_la", [128, T])
    cum = sb("e_cum", [128, T])
    ep = sb("e_ep", [128, T])
    en = sb("e_en", [128, T])
    dtx = sb("e_dtx", [128, T])
    scl = sb("e_scl", [128, T])
    sct = sb("e_sct", [LC, NT, 128])
    bt = sb("e_bt", [DS, T])
    ct = sb("e_ct", [DS, T])
    gm = sb("e_gm", [LC, NT, T])
    y = sb("e_y", [128, T])
    hn = sb("e_hn", [128, T])
    xf = sb("e_xf", [128, T])
    lg = sb("e_lg", [LC, NT, E])
    ex = sb("e_ex", [LC, NT, E])
    key = sb("e_key", [LC, NT, E])
    oh = sb("e_oh", [LC, NT, E])
    oh16 = sb("e_oh16", [LC, NT, E], BF16)
    cnt = sb("e_cnt", [LC, NT, E])
    m3 = sb("e_m3", [LC, 8, NT])
    wgt = sb("e_wgt", [LC, NT, E])
    wt = sb("e_wt", [E, T])
    run = sb("e_run", [LC, E])
    base = sb("e_base", [LC, NT, 128])
    acc = sb("e_acc", [LC, NT, 128])

    names = """h_loaded h_copied centered squared var_done rstd_ready normed xs_done zg_done xp_ready c_ready th_ready
        g_ready xs_ready sz_ready dt_done e_ready w1_ready lw_ready cum_ready ep_ready scl_ready turned
        sct_ready bc_done bt_ready ct_ready gram_done gm_ready y_done y_ready tail_done hn_ready logit_done
        lg_ready ex_ready oh_ready cnt_done wgt_ready wt_done wt_ready ident_done base_ready exp_done bank_read
        acc_ready dve_step act_step act_abs zeroed""".split()
    s = {n: sem("e_" + n) for n in names}
    s_out = sem("e_stored")
    STEPS = v.get("esteps", 0)

    with nc.Block() as block:
        @block.gpsimd
        def _(pool):
            pool.memset(xp[:, :], 0.0).then_inc(s["zeroed"], 1)
            pool.memset(run[:, :], 0.0).then_inc(s["zeroed"], 1)

        @block.sync
        def _(sp):
            for n in ("h_copied", "acc_ready"):
                sp.sem_inc(s[n], 1)
            sp.sem_inc(s_out, 16)
            with sp.Fori(0, B) as i:
                sp.wait_ge(s["h_copied"], i + 1)
                sp.dma_start(hin[:, :], h_d[bass.ds(i, 1)].rearrange("a p t -> p (a t)")).then_inc(s["h_loaded"], 16)
                sp.wait_ge(s["acc_ready"], i + 1 + 1)
                sp.dma_start(out[bass.ds(i, 1)].rearrange("a (c p) d -> p (a c) d", p=LC), acc[:, :, :])\
                  .then_inc(s_out, 16)
            sp.wait_ge(s_out, 16 * B + 16)

        @block.scalar
        def _(act):
            act.wait_ge(s["zeroed"], 2)
            with act.Fori(0, B) as i:
                step = Chain(act, s["act_step"], i, 3)

                def inverse_root(n, eps):
                    act.wait_ge(s["var_done"], 3 * i + n + 1)
                    step(act.activation(rstd[:, :], ps[:, 1, 0:T], ACT.Ln, bias=eps[:, 0:1]))
                    act.activation(rstd[:, :], rstd[:, :], ACT.Exp, scale=-0.5).then_inc(s["rstd_ready"], 1)

                act.wait_ge(s["centered"], 2 * i + 1)
                act.activation(sq[:, :], ps[:, 0, 0:T], ACT.Square).then_inc(s["squared"], 1)
                inverse_root(0, v["eps5"])
                act.wait_ge(s["normed"], 3 * i + 1)
                act.activation(sq[:, :], u[:, :], ACT.Square).then_inc(s["squared"], 1)
                inverse_root(1, v["eps6"])
                act.wait_ge(s["xs_done"], i + 1)
                act.activation(xp[:, 3:T + 3], ps[:, 2, 0:T], ACT.Copy).then_inc(s["xp_ready"], 1)
                act.wait_ge(s["zg_done"], i + 1)
                act.activation(th[:, 1, :], ps[:, 3, 0:T], ACT.Tanh, scale=0.5).then_inc(s["th_ready"], 1)
                act.activation(g[:, :, :], ps[:, 4:6, 0:T], ACT.Gelu).then_inc(s["g_ready"], 1)
                act.wait_ge(s["c_ready"], i + 1)
                act.activation(th[:, 0, :], c[:, :], ACT.Tanh, scale=0.5).then_inc(s["th_ready"], 1)
                act.wait_ge(s["bc_done"], i + 1)
                act.activation(bt[:, :], ps[0:DS, 4, 0:T], ACT.Copy).then_inc(s["bt_ready"], 1)
                act.activation(ct[:, :], ps[0:DS, 5, 0:T], ACT.Copy).then_inc(s["ct_ready"], 1)
                act.wait_ge(s["dt_done"], i + 1)
                act.activation(ee[:, :], ps[:, 6, 0:T], ACT.Abs, bias=col("b_dt")).then_inc(s["act_abs"], 1)
                act.wait_ge(s["act_abs"], i + 1)
                act.activation(ee[:, :], ee[:, :], ACT.Exp, scale=-1.0).then_inc(s["e_ready"], 1)
                act.wait_ge(s["w1_ready"], i + 1)
                act.activation(lw[:, :], w1[:, :], ACT.Ln).then_inc(s["lw_ready"], 1)
                act.wait_ge(s["cum_ready"], i + 1)
                act.activation(en[:, :], cum[:, :], ACT.Exp, scale=-1.0).then_inc(s["ep_ready"], 1)
                act.activation(ep[:, :], cum[:, :], ACT.Exp).then_inc(s["ep_ready"], 1)
                act.wait_ge(s["turned"], i + 1)
                act.activation(sct[:, :, :], ps[0:LC, 7, 0:384].rearrange("p (c d) -> p c d", c=NT), ACT.Copy)\
                   .then_inc(s["sct_ready"], 1)
                act.wait_ge(s["centered"], 2 * i + 2)
                act.activation(sq[:, :], ps[:, 0, 0:T], ACT.Square).then_inc(s["squared"], 1)
                inverse_root(2, v["eps5"])
                act.wait_ge(s["lg_ready"], i + 1)
                act.activation(ex[:, :, :], lg[:, :, :], ACT.Exp).then_inc(s["ex_ready"], 1)
                act.wait_ge(s["wt_done"], i + 1)
                act.activation(wt[:, :], ps[0:E, 4, 0:T], ACT.Copy).then_inc(s["wt_ready"], 1)
                act.wait_ge(s["ident_done"], i + 1)
                act.activation(base[:, :, :], ps[0:LC, 6, 0:384].rearrange("p (c d) -> p c d", c=NT), ACT.Copy)\
                   .then_inc(s["base_ready"], 1)
                step.end()

        @block.tensor
        def _(pe):
            pe.wait_ge(s["zeroed"], 2)
            with pe.Fori(0, B) as i:
                def mean_square(n):
                    pe.wait_ge(s["squared"], 3 * i + n + 1)
                    pe.matmul(ps[:, 1, 0:T], mean[:, :], sq[:, :], start=True, stop=True).then_inc(s["var_done"], 1)

                pe.wait_ge(s["h_copied"], i + 1 + 1)
                pe.matmul(ps[:, 0, 0:T], center[:, :], hb[:, :], start=True, stop=True).then_inc(s["centered"], 1)
                mean_square(0)
                mean_square(1)
                pe.wait_ge(s["normed"], 3 * i + 2)
                pe.matmul(ps[:, 2, 0:T], w_in[:, 0:128], xn[:, :], start=True, stop=True).then_inc(s["xs_done"], 1)
                pe.matmul(ps[:, 3, 0:T], w_in[:, 128:256], xn[:, :], start=True, stop=True)
                pe.matmul(ps[:, 4, 0:T], ffn1[:, 0:128], xn[:, :], start=True, stop=True)
                pe.matmul(ps[:, 5, 0:T], ffn1[:, 128:256], xn[:, :], start=True, stop=True).then_inc(s["zg_done"], 1)
                pe.wait_ge(s["xs_ready"], i + 1)
                pe.matmul(ps[:, 6, 0:T], w_dt[:, :], xs[:, :], start=True, stop=True).then_inc(s["dt_done"], 1)
                pe.wait_ge(s["g_ready"], i + 1)
                pe.matmul(ps[0:DS, 4, 0:T], w_b[:, :], xs[:, :], start=True, stop=True)
                pe.matmul(ps[0:DS, 5, 0:T], w_c[:, :], xs[:, :], start=True, stop=True).then_inc(s["bc_done"], 1)
                pe.wait_ge(s["bt_ready"], i + 1)
                pe.wait_ge(s["ct_ready"], i + 1)
                for k in range(NT):
                    a = LC * k
                    last = pe.matmul(ps[0:LC, k, a:T], bt[:, a:a + LC], ct[:, a:T], start=True, stop=True)
                last.then_inc(s["gram_done"], 1)
                pe.wait_ge(s["scl_ready"], i + 1)
                for k in range(NT):
                    last = pe.transpose(ps[0:LC, 7, 128 * k:128 * k + 128], scl[:, LC * k:LC * k + LC], ident[:, :])
                last.then_inc(s["turned"], 1)
                pe.wait_ge(s["sct_ready"], i + 1)
                pe.wait_ge(s["gm_ready"], i + 1)
                for k in range(NT):
                    last = pe.matmul(ps[:, 6, LC * k:T], sct[:, k, :], gm[:, k, LC * k:T], start=(k == 0),
                                     stop=(k == NT - 1), skip_group_check=True)
                last.then_inc(s["y_done"], 1)
                for k in range(2):
                    pe.matmul(ps[:, 7, 0:T], tail[:, 1 + k, :], g[:, k, :], start=(k == 0), stop=False)
                pe.wait_ge(s["y_ready"], i + 1)
                pe.matmul(ps[:, 7, 0:T], tail[:, 0, :], y[:, :], start=False, stop=True).then_inc(s["tail_done"], 1)

                pe.wait_ge(s["hn_ready"], i + 1)
                pe.matmul(ps[:, 0, 0:T], center[:, :], hn[:, :], start=True, stop=True).then_inc(s["centered"], 1)
                mean_square(2)
                pe.wait_ge(s["normed"], 3 * i + 3)
                for k in range(NT):
                    last = pe.matmul(ps[0:LC, 2, E * k:E * k + E], xf[:, LC * k:LC * k + LC], sw_t[:, :],
                                     start=True, stop=True)
                last.then_inc(s["logit_done"], 1)
                for k in range(NT):
                    last = pe.matmul(ps[0:LC, 5, 128 * k:128 * k + 128], xf[:, LC * k:LC * k + LC], ident[:, :],
                                     start=True, stop=True)
                pe.wait_ge(s["oh_ready"], i + 1)
                for k in range(NT + 1):
                    for m in range(min(k + 1, NT)):
                        last = pe.matmul(ps[0:LC, 3, E * k:E * k + E], (causal16 if m == k else ones16)[:, :],
                                         oh16[:, m, :], start=(m == 0), stop=(m == min(k, NT - 1)))
                last.then_inc(s["cnt_done"], 1)
                pe.wait_ge(s["wgt_ready"], i + 1)
                for k in range(NT):
                    last = pe.transpose(ps[0:E, 4, LC * k:LC * k + LC], wgt[:, k, :], ident[0:LC, 0:LC])
                last.then_inc(s["wt_done"], 1)
                pe.wait_ge(s["wt_ready"], i + 1)
                for k in range(NT):
                    a = slice(LC * k, LC * k + LC)
                    pe.matmul(ps[0:LC, 6, 128 * k:128 * k + 128], hn[:, a], ident[:, :], start=True, stop=False)
                    last = pe.matmul(ps[0:LC, 6, 128 * k:128 * k + 128], wt[:, a], eb[:, :], start=False, stop=True)
                last.then_inc(s["ident_done"], 1)
                for k in range(NT):
                    for n in range(4):
                        if k > 0:
                            pe.wait_ge(s["bank_read"], 12 * i + 4 * k + n - 3)
                        pe.matmul(ps[0:LC, n, :], xf[:, LC * k:LC * k + LC], ew_t[:, 512 * n:512 * n + 512],
                                  start=True, stop=True).then_inc(s["exp_done"], 1)

        @block.vector
        def _(dve):
            dve.wait_ge(s["zeroed"], 2)
            with dve.Fori(0, B) as i:
                step = Chain(dve, s["dve_step"], i, N_ESTEP)

                def bc(a):
                    return a.broadcast_to([LC, NT, E])

                dve.wait_ge(s["acc_ready"], i + 1)
                dve.wait_ge(s["h_loaded"], 16 * i + 16)
                dve.tensor_copy(hb[:, :], hin[:, :]).then_inc(s["h_copied"], 1)
                dve.wait_ge(s["rstd_ready"], 3 * i + 1)
                dve.tensor_tensor(u[:, :], ps[:, 0, 0:T], rstd[:, :], ALU.mult).then_inc(s["normed"], 1)
                dve.wait_ge(s["rstd_ready"], 3 * i + 2)
                dve.wait_ge(s["normed"], 3 * i + 1)
                dve.scalar_tensor_tensor(out=xn[:, :], in0=u[:, :], scalar=col("norm_w"), in1=rstd[:, :],
                                         op0=ALU.mult, op1=ALU.mult).then_inc(s["normed"], 1)
                dve.wait_ge(s["xp_ready"], i + 1)
                step(dve.tensor_scalar(c[:, :], xp[:, 0:T], vec[:, ACW:ACW + 1], col("aconv_b"), ALU.mult, ALU.add))
                for k in (1, 2, 3):
                    ins = dve.scalar_tensor_tensor(out=c[:, :], in0=xp[:, k:k + T], scalar=vec[:, ACW + k:ACW + k + 1],
                                                   in1=c[:, :], op0=ALU.mult, op1=ALU.add)
                    if k < 3:
                        step(ins)
                    else:
                        ins.then_inc(s["c_ready"], 1)
                dve.wait_ge(s["th_ready"], 2 * i + 1)
                step(dve.tensor_scalar(th[:, 1, :], th[:, 1, :], 0.5, 0.5, ALU.mult, ALU.add))
                dve.tensor_tensor(sz[:, :], th[:, 1, :], ps[:, 3, 0:T], ALU.mult).then_inc(s["sz_ready"], 1)
                dve.wait_ge(s["th_ready"], 2 * i + 2)
                step(dve.tensor_scalar(th[:, 0, :], th[:, 0, :], 0.5, 0.5, ALU.mult, ALU.add))
                dve.tensor_tensor(xs[:, :], th[:, 0, :], c[:, :], ALU.mult).then_inc(s["xs_ready"], 1)
                dve.wait_ge(s["e_ready"], i + 1)
                dve.tensor_scalar(w1[:, :], ee[:, :], 1.0, None, ALU.add).then_inc(s["w1_ready"], 1)
                step(dve.tensor_scalar(t2[:, :], ee[:, :], 0.5, -1.0, ALU.mult, ALU.add))
                dve.wait_ge(s["w1_ready"], i + 1)
                step(dve.scalar_tensor_tensor(out=t1[:, :], in0=w1[:, :], scalar=-1.0, in1=ee[:, :],
                                              op0=ALU.add, op1=ALU.subtract))
                step(dve.tensor_tensor(t1[:, :], t1[:, :], t2[:, :], ALU.mult))
                step(dve.tensor_scalar(t2[:, :], ps[:, 6, 0:T], col("b_dt"), 0.0, ALU.add, ALU.max))
                step(dve.tensor_tensor(dt[:, :], t2[:, :], t1[:, :], ALU.add))
                dve.wait_ge(s["lw_ready"], i + 1)
                step(dve.tensor_tensor(dt[:, :], dt[:, :], lw[:, :], ALU.add))
                step(dve.tensor_scalar(la[:, :], dt[:, :], neg_a[:, 0:1], -20.0, ALU.mult, ALU.max))
                step(dve.tensor_scalar(la[:, :], la[:, :], 20.0, None, ALU.min))
                dve.tensor_tensor_scan(cum[:, :], v["ones"][:, 0:T], la[:, :], 0.0, ALU.mult, ALU.add)\
                   .then_inc(s["cum_ready"], 1)
                step(dve.tensor_tensor(dtx[:, :], dt[:, :], xs[:, :], ALU.mult))
                dve.wait_ge(s["gram_done"], i + 1)
                for k in range(NT):
                    last = dve.tensor_tensor(gm[:, k, LC * k:T], ps[0:LC, k, LC * k:T], causal[:, 0:T - LC * k],
                                             ALU.mult)
                last.then_inc(s["gm_ready"], 1)
                dve.wait_ge(s["ep_ready"], 2 * i + 1)
                dve.tensor_tensor(scl[:, :], dtx[:, :], en[:, :], ALU.mult).then_inc(s["scl_ready"], 1)
                dve.wait_ge(s["ep_ready"], 2 * i + 2)
                dve.wait_ge(s["y_done"], i + 1)
                step(dve.tensor_tensor(y[:, :], ep[:, :], ps[:, 6, 0:T], ALU.mult))
                step(dve.scalar_tensor_tensor(out=y[:, :], in0=xs[:, :], scalar=col("D_param"), in1=y[:, :],
                                              op0=ALU.mult, op1=ALU.add))
                dve.tensor_tensor(y[:, :], y[:, :], sz[:, :], ALU.mult).then_inc(s["y_ready"], 1)
                dve.wait_ge(s["tail_done"], i + 1)
                step(dve.tensor_tensor(hn[:, :], ps[:, 7, 0:T], u[:, :], ALU.add))
                dve.tensor_tensor(hn[:, :], hn[:, :], hb[:, :], ALU.add).then_inc(s["hn_ready"], 1)
                dve.wait_ge(s["rstd_ready"], 3 * i + 3)
                dve.tensor_tensor(xf[:, :], ps[:, 0, 0:T], rstd[:, :], ALU.mult).then_inc(s["normed"], 1)

                negmax, total, inv, top, p, pos, kept, passed = (m3[:, k, :] for k in range(8))
                dve.wait_ge(s["logit_done"], i + 1)
                step(dve.tensor_tensor(lg[:, :, :], ps[0:LC, 2, 0:NT * E].rearrange("p (c e) -> p c e", c=NT),
                                       bc(sb_row[0:LC, None, :]), ALU.add))
                step(dve.tensor_reduce(negmax, lg[:, :, :], AX.X, ALU.max, negate=True))
                dve.tensor_tensor(lg[:, :, :], lg[:, :, :], bc(m3[:, 0, :, None]), ALU.add).then_inc(s["lg_ready"], 1)
                dve.wait_ge(s["ex_ready"], i + 1)
                step(dve.tensor_reduce(total, ex[:, :, :], AX.X, ALU.add))
                step(dve.tensor_reduce(top, ex[:, :, :], AX.X, ALU.max))
                step(dve.reciprocal(inv, total))
                step(dve.tensor_tensor(p, top, inv, ALU.mult))
                step(dve.tensor_tensor(key[:, :, :], ex[:, :, :], bc(m3[:, 3, :, None]), ALU.is_equal))
                step(dve.tensor_tensor(key[:, :, :], key[:, :, :], bc(tiebreak[:, None, :]), ALU.mult))
                step(dve.tensor_reduce(pos, key[:, :, :], AX.X, ALU.max))
                step(dve.tensor_tensor(oh[:, :, :], key[:, :, :], bc(m3[:, 5, :, None]), ALU.is_equal))
                dve.tensor_copy(oh16[:, :, :], oh[:, :, :]).then_inc(s["oh_ready"], 1)
                dve.wait_ge(s["cnt_done"], i + 1)
                step(dve.tensor_tensor(cnt[:, :, :], ps[0:LC, 3, 0:NT * E].rearrange("p (c e) -> p c e", c=NT),
                                       bc(run[:, None, :]), ALU.add))
                step(dve.tensor_tensor(run[:, :], run[:, :], ps[0:LC, 3, NT * E:NT * E + E], ALU.add))
                step(dve.tensor_tensor(cnt[:, :, :], cnt[:, :, :], oh[:, :, :], ALU.mult))
                step(dve.tensor_reduce(pos, cnt[:, :, :], AX.X, ALU.add))
                step(dve.tensor_scalar(kept, pos, float(CAP), None, ALU.is_le))
                step(dve.tensor_tensor(kept, kept, p, ALU.mult))
                step(dve.tensor_tensor(passed, p, kept, ALU.subtract))
                dve.tensor_tensor(wgt[:, :, :], oh[:, :, :], bc(m3[:, 6, :, None]), ALU.mult).then_inc(s["wgt_ready"], 1)
                dve.wait_ge(s["base_ready"], i + 1)
                dve.wait_ge(s["wgt_ready"], i + 1)
                dve.wait_ge(s_out, 16 * i + 16)
                for k in range(NT):
                    step(dve.scalar_tensor_tensor(out=acc[:, k, :], in0=ps[0:LC, 5, 128 * k:128 * k + 128],
                                                  scalar=passed[:, k:k + 1], in1=base[:, k, :],
                                                  op0=ALU.mult, op1=ALU.add))
                for k in range(NT):
                    for e in range(E):
                        if e % 4 == 0:
                            dve.wait_ge(s["exp_done"], 12 * i + 4 * k + e // 4 + 1)
                        ins = dve.scalar_tensor_tensor(out=acc[:, k, :],
                                                       in0=ps[0:LC, e // 4, 128 * (e % 4):128 * (e % 4) + 128],
                                                       scalar=wgt[:, k, e:e + 1], in1=acc[:, k, :],
                                                       op0=ALU.mult, op1=ALU.add)
                        if e % 4 < 3:
                            step(ins)
                        else:
                            ins.then_inc(s["bank_read"], 1)
                            dve.wait_ge(s["bank_read"], 12 * i + 4 * k + e // 4 + 1)
                    if k == NT - 1:
                        dve.nop().then_inc(s["acc_ready"], 1)
                step.end()


N_ESTEP = 73

_NAMES = {"q_w": "tok", "q_b": "tok", "k_w": "tok", "k_b": "tok", "v_w": "tok", "v_b": "tok", "o_w": "tok",
          "o_b": "tok", "ln1_g": "tok", "ln1_b": "tok", "f1_w": "tok", "f1_b": "tok", "f2_w": "tok",
          "f2_b": "tok", "ln2_g": "tok", "ln2_b": "tok", "conv_w": "tok", "conv_b": "tok",
          "norm_w": "attn", "W_in": "attn", "W_dt": "attn", "b_dt": "attn", "W_B": "attn",
          "W_C": "attn", "W_out": "attn", "log_A": "attn", "D_param": "attn", "W_ffn1": "attn",
          "W_ffn2": "attn", "W_merge": "attn",
          "switch_w": "ffn", "switch_b": "ffn", "expert_w": "ffn", "expert_b": "ffn"}
_INS = {short: f"L0_{block}_{short}" for short, block in _NAMES.items()}
_INS["aconv_w"] = "L0_attn_conv_w"
_INS["aconv_b"] = "L0_attn_conv_b"


def kernel(**inputs):
    import numpy as _np
    import concourse.bacc as _bacc
    from concourse import mybir as _mybir
    from concourse.bass_utils import run_bass_kernel_spmd as _run

    nc = _bacc.Bacc("TRN2", target_bir_lowering=False, num_devices=1)
    arrays, handles = {}, {}
    for short, name in [("x", "x"), *_INS.items()]:
        a = _np.ascontiguousarray(inputs[name])
        arrays[f"in_{name}"] = a
        handles[short] = nc.dram_tensor(f"in_{name}", a.shape, _mybir.dt.from_np(a.dtype), kind="ExternalInput").ap()
    out = nc.dram_tensor("out_0", (B, T, D), _mybir.dt.float32, kind="ExternalOutput").ap()
    build(nc, handles.pop("x"), handles, out)
    r = _run(nc, [arrays], core_ids=[0])
    return r.results[0]["out_0"]
```

```python
from contextlib import ExitStack

import numpy as np

import concourse.bass as bass
from concourse import mybir

F32 = mybir.dt.float32
BF16 = mybir.dt.bfloat16
ALU = mybir.AluOpType
ACT = mybir.ActivationFunctionType
AX = mybir.AxisListType

B, L, D = 32, 750, 128
H, HD = 8, 16
LC, NL = 125, 6
LH = L // 2
KTOP = int(L * 0.2)
NQ = H * KTOP
QC, NC = 120, 10
PQ = 2 * KTOP
F, NF = 512, 4
T, NT = 375, 3
DS = 32
E = 16
CAP = int(1.2 * B * T / E)
R = B * H
RG = R // 128
BIG = 16.0

VECS = ["q_b", "k_b", "v_b", "o_b", "ln1_g", "ln1_b", "f2_b", "ln2_g", "ln2_b", "conv_b",
        "norm_w", "aconv_b", "b_dt", "log_A", "D_param"]
F1B = len(VECS)
ACW = F1B + NF
NV = ACW + 4


SMALL_E = 2.0 ** -9

N_CONST = 8 + 1 + 3 * (H - 1) + 4 * 3 + 1 + 2 + 6


def later(count):
    return not isinstance(count, int) or count > 0


class Steps:

    def __init__(self, clip, per_clip, before=0):
        self.base, self.n, self.per_clip = clip * per_clip, before, per_clip

    def next(self):
        self.n += 1
        return self.base + self.n

    def end(self):
        assert self.n == self.per_clip, self.n


def build(nc, x, w, out):
    ctx = ExitStack()
    with ctx:
        def sb(name, shape, dt=F32):
            return ctx.enter_context(nc.sbuf_tensor(name, shape, dt))

        def sem(name):
            return ctx.enter_context(nc.semaphore(name))

        def dram(name, shape, dt):
            return nc.dram_tensor(name, shape, dt, kind="Internal").ap()

        norms_d = dram("norms_scratch", [R, L], F32)
        place_d = dram("place_scratch", [R, L], BF16)

        ps = ctx.enter_context(nc.psum_tensor("ps", [128, 8, 512], F32))

        ident = sb("ident", [128, 128])
        center = sb("center", [128, 128])
        mean = sb("mean", [128, 128])
        headsum = sb("headsum", [128, H])
        kept_iota = sb("kept_iota", [128, KTOP])
        place_of = sb("place_of", [128, NC])
        pair_mask = sb("pair_mask", [128, PQ])
        pair_scale = sb("pair_scale", [128, PQ])
        causal = sb("causal", [LC, T])
        causal16 = sb("causal16", [LC, LC], BF16)
        ones16 = sb("ones16", [LC, LC], BF16)
        tiebreak = sb("tiebreak", [LC, E])

        wqv = sb("wqv", [128, 256])
        wq, wv = wqv[:, 0:128], wqv[:, 128:256]
        wk, wo = (sb(n, [128, 128]) for n in ("wk", "wo"))
        f1w = sb("f1w", [128, F])
        f2c = sb("f2c", [128, NF, 128])
        cw = sb("cw", [128, 3, 128])
        vec = sb("vec", [128, NV])
        w_in = sb("w_in", [128, 2 * D])
        w_dt = sb("w_dt", [128, D])
        w_bc = sb("w_bc", [128, 2 * DS])
        ffn1 = sb("ffn1", [128, 2 * D])
        tail = sb("tail", [128, 3, D])
        sw_t = sb("sw_t", [128, E])
        ew_t = sb("ew_t", [128, E * 128])
        eb = sb("eb", [E, 128])
        sb_row = sb("sb_row", [128, E])
        neg_a = sb("neg_a", [128, 1])
        eps5 = sb("eps5", [128, 1])
        eps6 = sb("eps6", [128, 1])
        ones = sb("ones", [128, 1])
        f2_bc = sb("f2_bc", [128, 1])

        place_t = sb("place_t", [LC, NL, R], BF16)

        setup = ExitStack()

        def setup_sb(name, shape):
            return setup.enter_context(nc.sbuf_tensor(name, shape, F32))

        cw_raw = setup_sb("cw_raw", [128, 128, 3])
        vec_rows = setup_sb("vec_rows", [NV, 128])
        w_out = setup_sb("w_out", [128, D])
        ffn2 = setup_sb("ffn2", [128, 2, D])
        merge = setup_sb("merge", [128, 2, D])
        f2w = setup_sb("f2w", [128, NF, 128])
        f2t = setup_sb("f2t", [128, NF, 128])
        out_t = setup_sb("out_t", [128, 3, D])
        sw_rows = setup_sb("sw_rows", [E, 128])
        ew_raw = setup_sb("ew_raw", [128, E, 128])

        def col(name):
            k = VECS.index(name)
            return vec[:, k:k + 1]

        s_w = sem("weights_loaded")
        s_const = sem("constants_made")
        s_turned = sem("weights_turned")
        s_copied = sem("weights_copied")
        n_w = [0]

        with nc.Block() as block:
            @block.sync
            def _(sp):
                def load(dst, src):
                    sp.dma_start(dst, src).then_inc(s_w, 16)
                    n_w[0] += 16
                for k, name in enumerate(VECS):
                    load(vec_rows[k:k + 1, :], w[name].rearrange("(a d) -> a d", a=1))
                load(vec_rows[F1B:F1B + NF, :], w["f1_b"].rearrange("(a d) -> a d", a=NF))
                load(vec[:, ACW:ACW + 4], w["aconv_w"].rearrange("d a k -> d (a k)"))
                for dst, name in ((wq, "q_w"), (wk, "k_w"), (wv, "v_w"), (wo, "o_w"), (f1w, "f1_w"),
                                  (w_in, "W_in"), (w_dt, "W_dt"), (w_bc[:, 0:DS], "W_B"), (w_bc[:, DS:2 * DS], "W_C"),
                                  (w_out, "W_out"), (ffn1, "W_ffn1"), (sw_rows, "switch_w"), (eb, "expert_b")):
                    load(dst[:, :], w[name])
                load(f2w[:, :, :], w["f2_w"].rearrange("(c p) n -> p c n", p=128))
                load(ffn2[:, :, :], w["W_ffn2"].rearrange("(c p) n -> p c n", p=128))
                load(merge[:, :, :], w["W_merge"].rearrange("(c p) n -> p c n", p=128))
                load(cw_raw[:, :, :], w["conv_w"])
                load(ew_raw[:, :, :], w["expert_w"].rearrange("e f d -> f e d"))
                load(sb_row[:, :], w["switch_b"].rearrange("(a e) -> a e", a=1).broadcast_to([128, E]))

            @block.gpsimd
            def _(pool):
                chain = [0]

                def made(ins):
                    ins.then_inc(s_const, 1)
                    chain[0] += 1
                    pool.wait_ge(s_const, chain[0])

                made(pool.memset(ident[:, :], 0.0))
                made(pool.affine_select(out=ident[:, :], in_=ident[:, :], compare_op=ALU.not_equal, fill=1.0,
                                        base=0, pattern=[[-1, 128]], channel_multiplier=1))
                made(pool.memset(mean[:, :], 1.0 / D))
                made(pool.tensor_tensor(center[:, :], ident[:, :], mean[:, :], ALU.subtract))
                made(pool.memset(headsum[:, :], 1.0))
                made(pool.affine_select(out=headsum[:, :], in_=headsum[:, :], compare_op=ALU.is_ge, fill=0.0,
                                        base=0, pattern=[[-HD, H]], channel_multiplier=1))
                made(pool.affine_select(out=headsum[:, :], in_=headsum[:, :], compare_op=ALU.is_ge, fill=0.0,
                                        base=HD - 1, pattern=[[HD, H]], channel_multiplier=-1))
                made(pool.iota(kept_iota[:, :], pattern=[[1, KTOP]], base=1, channel_multiplier=0,
                               allow_small_or_imprecise_dtypes=True))
                made(pool.iota(place_of[:, :], pattern=[[QC, NC]], base=1, channel_multiplier=1,
                               allow_small_or_imprecise_dtypes=True))
                step = pair_scale[:, 0:NC]
                for h in range(1, H):
                    made(pool.memset(step, -float(KTOP)))
                    made(pool.affine_select(out=step, in_=step, compare_op=ALU.is_ge, fill=0.0,
                                            base=-KTOP * h, pattern=[[QC, NC]], channel_multiplier=1))
                    made(pool.tensor_tensor(place_of[:, :], place_of[:, :], step, ALU.add))
                for i in range(4):
                    half = pair_mask[32 * i:32 * i + 32, :]
                    made(pool.memset(half, 1.0))
                    first, last = half[:, 0:KTOP], half[:, KTOP:PQ]
                    made(pool.affine_select(out=first, in_=first, compare_op=ALU.is_ge, fill=0.0,
                                            base=HD - 1, pattern=[[0, KTOP]], channel_multiplier=-1))
                    made(pool.affine_select(out=last, in_=last, compare_op=ALU.is_ge, fill=0.0,
                                            base=-HD, pattern=[[0, KTOP]], channel_multiplier=1))
                made(pool.tensor_scalar(pair_scale[:, :], pair_mask[:, :], HD ** -0.5, None, ALU.mult))
                made(pool.memset(causal[:, :], 1.0))
                made(pool.affine_select(out=causal[:, :], in_=causal[:, :], compare_op=ALU.is_ge, fill=0.0,
                                        base=0, pattern=[[1, T]], channel_multiplier=-1))
                made(pool.tensor_copy(causal16[:, :], causal[:, 0:LC]))
                made(pool.memset(ones16[:, :], 1.0))
                made(pool.memset(eps5[:, :], 1e-5))
                made(pool.memset(eps6[:, :], 1e-6))
                made(pool.memset(ones[:, :], 1.0))
                made(pool.iota(tiebreak[:, :], pattern=[[-1, E]], base=E, channel_multiplier=0,
                               allow_small_or_imprecise_dtypes=True))
                assert chain[0] == N_CONST, chain[0]

            @block.tensor
            def _(pe):
                pe.wait_ge(s_const, N_CONST)
                pe.wait_ge(s_w, n_w[0])
                pe.transpose(ps[:, 0, 0:ACW], vec_rows[0:ACW, :], ident[0:ACW, 0:ACW])
                for k in range(3):
                    pe.transpose(ps[:, 1, 128 * k:128 * k + 128], cw_raw[:, :, k], ident[:, :])
                pe.transpose(ps[:, 2, 0:128], w_out[:, :], ident[:, :])
                for k in range(2):
                    pe.transpose(ps[:, 2, 128 * k + 128:128 * k + 256], ffn2[:, k, :], ident[:, :])
                pe.transpose(ps[:, 0, 64:64 + E], sw_rows[:, :], ident[0:E, 0:E])
                for k in range(NF):
                    pe.transpose(ps[:, 3, 128 * k:128 * k + 128], f2w[:, k, :], ident[:, :])
                for e in range(E):
                    last = pe.transpose(ps[:, 4 + e // 4, 128 * (e % 4):128 * (e % 4) + 128], ew_raw[:, e, :],
                                        ident[:, :])
                last.then_inc(s_turned, 1)
                pe.wait_ge(s_copied, 5)
                for k in range(NF):
                    pe.matmul(ps[:, 1, 128 * k:128 * k + 128], f2t[:, k, :], center[:, :], start=True, stop=True)
                pe.matmul(ps[:, 2, 0:1], center[:, :], col("f2_b"), start=True, stop=True)
                for k in range(3):
                    last = pe.matmul(ps[:, 0, 128 * k:128 * k + 128], out_t[:, k, :],
                                     merge[:, 0 if k == 0 else 1, :], start=True, stop=True)
                last.then_inc(s_turned, 1)

            @block.vector
            def _(dve):
                dve.wait_ge(s_turned, 1)
                dve.tensor_copy(vec[:, 0:ACW], ps[:, 0, 0:ACW]).then_inc(s_copied, 1)
                dve.tensor_copy(cw[:, :, :], ps[:, 1, 0:384].rearrange("p (k n) -> p k n", k=3)).then_inc(s_copied, 1)
                dve.tensor_copy(out_t[:, :, :], ps[:, 2, 0:384].rearrange("p (k n) -> p k n", k=3))\
                   .then_inc(s_copied, 1)
                dve.tensor_copy(f2t[:, :, :], ps[:, 3, :].rearrange("p (k n) -> p k n", k=NF)).then_inc(s_copied, 1)
                dve.tensor_copy(sw_t[:, :], ps[:, 0, 64:64 + E]).then_inc(s_copied, 1)
                for k in range(4):
                    dve.tensor_copy(ew_t[:, 512 * k:512 * k + 512], ps[:, 4 + k, :]).then_inc(s_copied, 1)
                dve.wait_ge(s_turned, 2)
                dve.tensor_copy(f2c[:, :, :], ps[:, 1, :].rearrange("p (k n) -> p k n", k=NF)).then_inc(s_copied, 1)
                dve.tensor_copy(f2_bc[:, :], ps[:, 2, 0:1]).then_inc(s_copied, 1)
                dve.tensor_copy(tail[:, :, :], ps[:, 0, 0:384].rearrange("p (k n) -> p k n", k=3))\
                   .then_inc(s_copied, 1)

            @block.scalar
            def _(act):
                act.wait_ge(s_copied, 1)
                act.activation(neg_a[:, :], col("log_A"), ACT.Exp).then_inc(s_a := sem("a_exp"), 1)
                act.wait_ge(s_a, 1)
                act.mul(neg_a[:, :], neg_a[:, :], -1.0).then_inc(s_a, 1)
                act.wait_ge(s_a, 2)

        setup.close()

        with ExitStack() as part, nc.Block() as block:
            xin = part.enter_context(nc.sbuf_tensor("a_xin", [LC, 2, NL, 128], F32))
            xt = part.enter_context(nc.sbuf_tensor("a_xt", [128, 2, 2, LH], F32))
            sq = part.enter_context(nc.sbuf_tensor("a_sq", [128, 2, 2, LH], F32))
            nrm = part.enter_context(nc.sbuf_tensor("a_nrm", [H, 2, 2, LH], F32))
            s_in = [sem(f"a_x_loaded{k}") for k in range(2)]
            s_xt = sem("a_x_turned")
            s_xc = sem("a_xt_ready")
            s_q = sem("a_q_done")
            s_sq = sem("a_squares_ready")
            s_n = sem("a_norms_done")
            s_nc = sem("a_norms_ready")
            s_no = [sem(f"a_norms_stored{k}") for k in range(2)]

            @block.sync
            def _(sp):
                def load(j, k):
                    if later(j - 1):
                        sp.wait_ge(s_xt, j - 1)
                    sp.dma_start(xin[:, k], x[bass.ds(j, 1)].rearrange("a (c p) d -> p (a c) d", p=LC))\
                      .then_inc(s_in[k], 16)

                def store(j, k):
                    sp.wait_ge(s_nc, j + 1)
                    sp.dma_start(norms_d[bass.ds(H * j, H), :].rearrange("h (n l) -> h n l", n=2), nrm[:, k])\
                      .then_inc(s_no[k], 16)

                for k in range(2):
                    load(k, k)
                with sp.Fori(1, B // 2) as i:
                    for k in range(2):
                        load(2 * i + k, k)
                        store(2 * i + k - 2, k)
                for k in range(2):
                    store(B - 2 + k, k)
                for k in range(2):
                    sp.wait_ge(s_no[k], 16 * (B // 2))

            @block.tensor
            def _(pe):
                def turn_x(j, k, i):
                    pe.wait_ge(s_in[k], 16 * i + 16)
                    if later(j):
                        pe.wait_ge(s_xc, j)
                    for c in range(NL):
                        last = pe.transpose(ps[:, c // 3, LC * (c % 3):LC * (c % 3) + LC], xin[:, k, c, :],
                                            ident[0:LC, 0:LC])
                    last.then_inc(s_xt, 1)

                def queries(j, k):
                    pe.wait_ge(s_xc, j + 1)
                    if later(j):
                        pe.wait_ge(s_sq, j)
                    for n in range(2):
                        last = pe.matmul(ps[:, 2 + n, 0:LH], wq, xt[:, k, n, :], start=True, stop=True)
                    last.then_inc(s_q, 1)

                def norms(j, k):
                    pe.wait_ge(s_sq, j + 1)
                    if later(j):
                        pe.wait_ge(s_nc, j)
                    for n in range(2):
                        last = pe.matmul(ps[0:H, 4 + n, 0:LH], headsum[:, :], sq[:, k, n, :], start=True, stop=True)
                    last.then_inc(s_n, 1)

                def pair(i, more=True):
                    queries(2 * i, 0)
                    turn_x(2 * i + 1, 1, i)
                    norms(2 * i, 0)
                    queries(2 * i + 1, 1)
                    if more:
                        turn_x(2 * i + 2, 0, i + 1)
                    norms(2 * i + 1, 1)

                turn_x(0, 0, 0)
                pair(0)
                with pe.Fori(1, B // 2 - 1) as i:
                    pair(i)
                pair(B // 2 - 1, more=False)

            @block.scalar
            def _(act):
                def pair(i):
                    for k in range(2):
                        act.wait_ge(s_q, 2 * i + k + 1)
                        if later(2 * i + k - 1):
                            act.wait_ge(s_n, 2 * i + k - 1)
                        act.activation(sq[:, k], ps[:, 2:4, 0:LH], ACT.Square, bias=col("q_b")).then_inc(s_sq, 1)

                pair(0)
                with act.Fori(1, B // 2) as i:
                    pair(i)

            @block.vector
            def _(dve):
                def copy_x(j, k):
                    dve.wait_ge(s_xt, j + 1)
                    if later(j - 1):
                        dve.wait_ge(s_q, j - 1)
                    dve.tensor_copy(xt[:, k], ps[:, 0:2, 0:LH]).then_inc(s_xc, 1)

                def copy_norms(j, k, i):
                    dve.wait_ge(s_n, j + 1)
                    if later(16 * i):
                        dve.wait_ge(s_no[k], 16 * i)
                    dve.tensor_copy(nrm[:, k], ps[0:H, 4:6, 0:LH]).then_inc(s_nc, 1)

                def pair(i, more=True):
                    copy_x(2 * i + 1, 1)
                    copy_norms(2 * i, 0, i)
                    if more:
                        copy_x(2 * i + 2, 0)
                    copy_norms(2 * i + 1, 1, i)

                copy_x(0, 0)
                pair(0)
                with dve.Fori(1, B // 2 - 1) as i:
                    pair(i)
                pair(B // 2 - 1, more=False)

        with ExitStack() as part, nc.Block() as block:
            work = part.enter_context(nc.sbuf_tensor("k_work", [128, RG, L], F32))
            mask = part.enter_context(nc.sbuf_tensor("k_mask", [128, RG, L], F32))
            count = part.enter_context(nc.sbuf_tensor("k_count", [128, RG, L], F32))
            place = part.enter_context(nc.sbuf_tensor("k_place", [128, RG, L], F32))
            place16 = part.enter_context(nc.sbuf_tensor("k_place16", [128, RG, L], BF16))
            top8 = part.enter_context(nc.sbuf_tensor("k_top8", [128, RG, 8], F32))
            s_l = sem("k_norms_loaded")
            s_m = [sem(f"k_max_found{g}") for g in range(RG)]
            s_r = [sem(f"k_max_removed{g}") for g in range(RG)]
            s_k = sem("k_step")
            s_seen = sem("k_wait_seen")
            s_t = sem("k_places_turned")
            s_tc = sem("k_places_copied")
            s_p16 = sem("k_places16_ready")
            s_ps = sem("k_places_stored")
            FULL = KTOP // 8

            @block.sync
            def _(sp):
                sp.dma_start(work[:, :, :], norms_d.rearrange("(g p) l -> p g l", p=128)).then_inc(s_l, 16)
                sp.wait_ge(s_p16, RG)
                sp.dma_start(place_d.rearrange("(g p) l -> p g l", p=128), place16[:, :, :]).then_inc(s_ps, 16)
                sp.wait_ge(s_ps, 16)

            @block.vector
            def _(dve):
                dve.wait_ge(s_l, 16)
                def find(i, g):
                    if later(i):
                        dve.wait_ge(s_r[g], i)
                    if not isinstance(i, int):
                        dve.sem_inc(s_seen, 1)
                    dve.max(top8[:, g, :], work[:, g, :]).then_inc(s_m[g], 1)

                def remove(i, g):
                    dve.wait_ge(s_m[g], i + 1)
                    if not isinstance(i, int):
                        dve.sem_inc(s_seen, 1)
                    dve.match_replace(work[:, g, :], top8[:, g, :], work[:, g, :], -1.0).then_inc(s_r[g], 1)

                for g in range(RG):
                    find(0, g)
                for g in range(RG):
                    remove(0, g)
                with dve.Fori(1, FULL) as i:
                    for g in range(RG):
                        find(i, g)
                    for g in range(RG):
                        remove(i, g)
                for g in range(RG):
                    find(FULL, g)
                for g in range(RG):
                    dve.wait_ge(s_m[g], FULL + 1)
                    dve.memset(top8[:, g, KTOP % 8:8], -1.0).then_inc(s_m[g], 1)
                for g in range(RG):
                    dve.wait_ge(s_m[g], FULL + 2)
                    dve.match_replace(work[:, g, :], top8[:, g, :], work[:, g, :], -1.0).then_inc(s_r[g], 1)
                n = 0
                for g in range(RG):
                    dve.wait_ge(s_r[g], FULL + 1)
                    dve.tensor_scalar(mask[:, g, :], work[:, g, :], 0.0, None, ALU.is_lt).then_inc(s_k, 1)
                    n += 1
                for g in range(RG):
                    dve.wait_ge(s_k, g + 1)
                    dve.tensor_tensor_scan(count[:, g, :], mask[:, g, :], mask[:, g, :], 0.0, ALU.add, ALU.max)\
                       .then_inc(s_k, 1)
                for g in range(RG):
                    dve.wait_ge(s_k, RG + g + 1)
                    dve.tensor_tensor(place[:, g, :], count[:, g, :], mask[:, g, :], ALU.mult).then_inc(s_k, 1)
                for g in range(RG):
                    dve.wait_ge(s_k, 2 * RG + g + 1)
                    dve.tensor_copy(place16[:, g, :], place[:, g, :]).then_inc(s_p16, 1)
                for c in range(NL):
                    dve.wait_ge(s_t, c + 1)
                    dve.tensor_copy(place_t[:, c, :], ps[0:LC, c, 0:R]).then_inc(s_tc, 1)

            @block.tensor
            def _(pe):
                pe.wait_ge(s_k, 3 * RG)
                for c in range(NL):
                    for g in range(RG):
                        last = pe.transpose(ps[0:LC, c, 128 * g:128 * g + 128], place[:, g, LC * c:LC * c + LC],
                                            ident[:, :])
                    last.then_inc(s_t, 1)

        with ExitStack() as part:
            layers(nc, part, locals())


def layers(nc, part, v):
    ps, ident, center, mean, vec = v["ps"], v["ident"], v["center"], v["mean"], v["vec"]
    wq, wk, wv, wqv, wo, f1w, f2c, f2_bc, cw = (v[n] for n in ("wq", "wk", "wv", "wqv", "wo", "f1w", "f2c", "f2_bc", "cw"))
    pair_mask, pair_scale, kept_iota, place_of = (v[n] for n in ("pair_mask", "pair_scale", "kept_iota", "place_of"))
    w_in, w_dt, w_bc, ffn1, tail = (v[n] for n in ("w_in", "w_dt", "w_bc", "ffn1", "tail"))
    sw_t, ew_t, eb, sb_row, neg_a = (v[n] for n in ("sw_t", "ew_t", "eb", "sb_row", "neg_a"))
    causal, causal16, ones16, tiebreak, ones = (v[n] for n in ("causal", "causal16", "ones16", "tiebreak", "ones"))
    place_t, place_d, x, out, col, sem = (v[n] for n in ("place_t", "place_d", "x", "out", "col", "sem"))
    eps5, eps6 = v["eps5"], v["eps6"]

    def sb(name, shape, dt=F32):
        return part.enter_context(nc.sbuf_tensor(name, shape, dt))

    xin = sb("xin", [LC, NL, 128])
    xt = sb("xt", [128, 2, LH])
    xc = sb("xc", [128, 2, LH])
    xmean = sb("xmean", [128, 1])
    qb = sb("qb", [128, 1])
    mv = sb("mv", [128, 1])
    mo = sb("mo", [128, 1])
    kt = sb("kt", [128, 2, LH])
    vtok = sb("vtok", [LC, NL, 128])
    pick = sb("pick", [LC, NL, NQ])
    place = sb("place", [LC, NL, H])
    spread = sb("spread", [QC, NC, L], BF16)
    blk = sb("blk", [128, NQ])
    ablk = blk
    prob = sb("prob", [QC, 2, L])
    probt = sb("probt", [LC, NL, NQ])
    nmax = sb("nmax", [QC, NC])
    den = sb("den", [QC, NC])
    rden = sb("rden", [QC, NC])
    q_z = sb("q_z", [128, NC, 128])
    qtok = q_z[0:LC, 0:NL, :]
    z = q_z[0:QC, :, :]
    zpart = [sb(f"zpart{k}", [QC, NC, 128], BF16) for k in range(3)]
    ao = sb("ao", [128, 2, LH])
    res = sb("res", [128, 2, LH])
    cen = sb("cen", [128, 2, LH])
    hid = cen
    bsq = sb("bsq", [128, 2, LH])
    ff = sb("ff", [128, NF, 2, LH])
    fused = sb("fused", [128, L + 2])
    pooled = sb("pooled", [128, T])
    part_rows = ff[0:LC, :, :, :].rearrange("p k n l -> p (k n l)")[:, 0:2048].rearrange("p (s e d) -> p s e d", s=2, e=8)
    hb = sb("hb", [128, T])
    csq = sb("csq", [128, T])
    u = sb("u", [128, T])
    xn = sb("xn", [128, T])
    xp = sb("xp", [128, T + 3])
    c_ = sb("c", [128, T])
    xs_sz = sb("xs_sz", [128, 2, T])
    xs, sz = xs_sz[:, 0, :], xs_sz[:, 1, :]
    g = sb("g", [128, 2, T])
    ee_ep = sb("ee_ep", [128, T])
    w1_cum = sb("w1_cum", [128, T])
    lw_la = sb("lw_la", [128, T])
    t1_y = sb("t1_y", [128, T])
    t2_en = sb("t2_en", [128, T])
    dt = sb("dt", [128, T])
    dtx = sb("dtx", [128, T])
    sct = sb("sct", [LC, NT, 128])
    bt = sb("bt", [DS, T])
    ct = sb("ct", [DS, T])
    gm = sb("gm", [LC, NT, T])
    hn = sb("hn", [128, T])
    xf = sb("xf", [128, T])
    lg = sb("lg", [LC, NT, E])
    ex = sb("ex", [LC, NT, E])
    key = sb("key", [LC, NT, E])
    oh = sb("oh", [LC, NT, E])
    oh16 = sb("oh16", [LC, NT, E], BF16)
    cnt = sb("cnt", [LC, NT, E])
    m3 = sb("m3", [LC, 8, NT])
    wgt = sb("wgt", [LC, NT, E])
    wt = bt[0:E, :]
    run = sb("run", [LC, E])
    base = sct
    acc = sb("acc", [LC, NT, 128])

    def sems(names):
        return {n: sem(n) for n in names.split()}

    sA = sems("""x_loaded x_turned xt_ready mean_ready k_done qv_done means_done kt_ready q_ready v_ready qb_ready
        mv_ready mo_done mo_ready place_ready pick_ready gathered blk_ready scored max_ready prob_ready
        prob_turned probt_dve probt_act av_done ablk_ready z_done z_ready z_parts z_res z_part2 place_loaded
        spread_ready spread_done ao_ready x_kept res_ready a_dve pool_seen zeroed""")
    sB = sems("""center1 cen1 squared1 var1 rstd1 hid1 f1_done ff_act ff_dve center2 cen2 squared2 var2 rstd2
        hid2 fused_ready conv_done pooled_ready h_ready b_dve b_act""")
    sC = sems("""c_center c_squared c_var c_rstd u_ready xn_ready xs_done z_proj xp_ready th_z sz_ready g_done g_ready
        c_ready th_c xs_ready dt_done abs_ready e_ready dt_max w1_ready lw_ready cum_ready en_ready ep_ready bc_done
        bt_ready ct_ready gram_done gm_ready scl_ready scl_turned sct_ready y_done y_ready tail_done hn_ready
        xf_ready logit_done lg_ready ex_ready oh_ready cnt_done wgt_ready wt_done wt_ready own_done base_done
        base_ready own_ready exp_done even_read odd_read weighted summed c_pool acc_ready rows_ready c_dve c_act stored""")

    runs = []
    for c in range(NC // 2):
        q = QC * c
        while q < QC * (c + 1):
            h = q // KTOP
            n = min(KTOP * (h + 1), QC * (c + 1)) - q
            runs.append((c, q - QC * c, n, h))
            q += n

    def turns(turn, eng, extra=0):
        turn(0, None, None)
        turn(1, 0, None)
        turn(2, 1, 0)
        with eng.Fori(3, B - 1) as i:
            turn(i, i - 1, i - 2)
        turn(B - 1, B - 2, B - 3, more=False)
        turn(None, B - 1, B - 2)
        turn(None, None, B - 1)

    with nc.Block() as block:
        @block.sync
        def _(sp):
            def load_x(a):
                if later(a):
                    sp.wait_ge(sA["x_turned"], a)
                sp.dma_start(xin[:, :, :], x[bass.ds(a, 1)].rearrange("a (c p) d -> p (a c) d", p=LC))\
                  .then_inc(sA["x_loaded"], 16)

            def load_places(a):
                if later(a):
                    sp.wait_ge(sA["spread_done"], a)
                for c, p, n, h in runs:
                    src = place_d[bass.ds(H * a, H), :].rearrange("(a h) l -> h a l", a=2)[h:h + 1]
                    sp.dma_start(spread[p:p + n, c::NC // 2, :], src.broadcast_to([n, 2, L]))\
                      .then_inc(sA["place_loaded"], 16)

            def turn(a, b, c, more=True):
                if a is not None and more:
                    load_x(a + 1)
                    load_places(a + 1)
                if c is not None:
                    sp.wait_ge(sC["rows_ready"], NT * c + NT)
                    sp.dma_start(out[bass.ds(c, 1)].rearrange("a (c p) d -> p (a c) d", p=LC), acc[:, :, :])\
                      .then_inc(sC["stored"], 16)

            load_x(0)
            load_places(0)
            turns(turn, sp)
            sp.wait_ge(sC["stored"], 16 * B)

        @block.gpsimd
        def _(pool):
            for one in (blk, fused, xp, run):
                pool.memset(one[:, :], 0.0).then_inc(sA["zeroed"], 1)

            def picks(a):
                pool.wait_ge(sA["place_ready"], a + 1)
                if later(a):
                    pool.wait_ge(sA["gathered"], a)
                if not isinstance(a, int):
                    pool.sem_inc(sA["pool_seen"], 1)
                for c in range(NL):
                    for h in range(H):
                        last = pool.tensor_scalar(pick[:, c, KTOP * h:KTOP * h + KTOP], kept_iota[0:LC, :],
                                                  place[:, c, h:h + 1], None, ALU.is_equal)
                    last.then_inc(sA["pick_ready"], 1)

            def keep_x(a):
                pool.wait_ge(sA["xt_ready"], a + 1)
                if later(a):
                    pool.wait_ge(sB["center1"], a)
                if not isinstance(a, int):
                    pool.sem_inc(sA["pool_seen"], 1)
                pool.tensor_copy(res[:, :, :], xt[:, :, :]).then_inc(sA["x_kept"], 1)

            def sum_rows(c, k, steps):
                rows = part_rows[:, k % 2]
                pool.wait_ge(sC["odd_read"], 6 * c + 2 * k + 2)
                pool.tensor_tensor(rows[:, 0:4, :], rows[:, 0:4, :], rows[:, 4:8, :], ALU.add).then_inc(sC["c_pool"], 1)
                pool.wait_ge(sC["c_pool"], steps.next())
                pool.tensor_tensor(rows[:, 0:2, :], rows[:, 0:2, :], rows[:, 2:4, :], ALU.add).then_inc(sC["c_pool"], 1)
                pool.wait_ge(sC["c_pool"], steps.next())
                pool.tensor_tensor(rows[:, 0, :], rows[:, 0, :], rows[:, 1, :], ALU.add).then_inc(sC["summed"], 1)
                pool.wait_ge(sC["summed"], NT * c + k + 1)
                pool.wait_ge(sC["acc_ready"], NT * c + k + 1)
                pool.tensor_tensor(acc[:, k, :], acc[:, k, :], rows[:, 0, :], ALU.add).then_inc(sC["rows_ready"], 1)

            def turn(a, b, c, more=True):
                if a is not None:
                    keep_x(a)
                if a is not None and more:
                    picks(a + 1)
                if c is not None:
                    steps = Steps(c, 2 * NT)
                    for k in range(NT):
                        sum_rows(c, k, steps)
                    steps.end()

            picks(0)
            turns(turn, pool)

        @block.tensor
        def _(pe):
            pe.wait_ge(sA["zeroed"], 4)

            def turn_x(a):
                pe.wait_ge(sA["x_loaded"], 16 * a + 16)
                if later(a):
                    pe.wait_ge(sA["z_ready"], a)
                for c in range(NL):
                    last = pe.transpose(ps[:, c // 3, LC * (c % 3):LC * (c % 3) + LC], xin[:, c, :],
                                        ident[0:LC, 0:LC])
                last.then_inc(sA["x_turned"], 1)

            def keys(a):
                pe.wait_ge(sA["xt_ready"], a + 1)
                if later(a):
                    pe.wait_ge(sA["ao_ready"], a)
                for n in range(2):
                    last = pe.matmul(ps[:, 2 + n, 0:LH], wk[:, :], xt[:, n, :], start=True, stop=True)
                last.then_inc(sA["k_done"], 1)

            def queries_values(a):
                pe.wait_ge(sA["mean_ready"], a + 1)
                flat = xc[:, :, :].rearrange("p n l -> p (n l)")
                for c in range(NL):
                    if c == 4:
                        pe.wait_ge(sA["kt_ready"], a + 1)
                    last = pe.matmul(ps[0:LC, c // 2, 256 * (c % 2):256 * (c % 2) + 256],
                                     flat[:, LC * c:LC * c + LC], wqv[:, :], start=True, stop=True)
                last.then_inc(sA["qv_done"], 1)
                pe.matmul(ps[:, 3, 0:1], wq, xmean[:, 0:1], start=True, stop=True)
                pe.matmul(ps[:, 3, 1:2], wv, xmean[:, 0:1], start=True, stop=True).then_inc(sA["means_done"], 1)

            def mean_out(a):
                pe.wait_ge(sA["mv_ready"], a + 1)
                pe.wait_ge(sA["qb_ready"], a + 1)
                pe.matmul(ps[:, 3, 2:3], wo[:, :], mv[:, 0:1], start=True, stop=True).then_inc(sA["mo_done"], 1)

            def gather(a):
                pe.wait_ge(sA["q_ready"], a + 1)
                pe.wait_ge(sA["v_ready"], a + 1)
                for c in range(NL):
                    pe.wait_ge(sA["pick_ready"], NL * a + c + 1)
                    for j in range(4):
                        last = pe.matmul(ps[32 * j:32 * j + 32, 0, 0:PQ], qtok[:, c, 32 * j:32 * j + 32],
                                         pick[:, c, PQ * j:PQ * j + PQ], start=(c == 0), stop=(c == NL - 1),
                                         skip_group_check=True)
                last.then_inc(sA["gathered"], 1)

            def scores(a, c):
                if c == 0:
                    pe.wait_ge(sA["blk_ready"], a + 1)
                else:
                    pe.wait_ge(sA["prob_ready"], NC * a + c)
                for n in range(2):
                    last = pe.matmul(ps[0:QC, n, 0:LH], blk[:, QC * c:QC * c + QC], kt[:, n, :],
                                     start=True, stop=True)
                last.then_inc(sA["scored"], 1)

            def turn_probs(a, c):
                pe.wait_ge(sA["prob_ready"], NC * a + c + 1)
                if c == 0:
                    pe.wait_ge(sA["mo_ready"], a + 1)
                    if later(2 * a - 2):
                        pe.wait_ge(sC["g_ready"], 2 * a - 2)
                else:
                    pe.wait_ge(sA["probt_dve"], NC * a + c)
                    pe.wait_ge(sA["probt_act"], NC * a + c)
                for m in range(NL):
                    last = pe.transpose(ps[0:LC, 2 + m // 3, QC * (m % 3):QC * (m % 3) + QC],
                                        prob[:, c % 2, LC * m:LC * m + LC], ident[0:QC, 0:QC])
                last.then_inc(sA["prob_turned"], 1)

            def attend(a):
                pe.wait_ge(sA["probt_dve"], NC * a + NC)
                pe.wait_ge(sA["probt_act"], NC * a + NC)
                for c in range(NL):
                    for j in range(4):
                        last = pe.matmul(ps[32 * j:32 * j + 32, 0, 0:PQ], vtok[:, c, 32 * j:32 * j + 32],
                                         probt[:, c, PQ * j:PQ * j + PQ], start=(c == 0), stop=(c == NL - 1),
                                         skip_group_check=True)
                last.then_inc(sA["av_done"], 1)

            def attend_out(a):
                pe.wait_ge(sA["ablk_ready"], a + 1)
                for c in range(NC):
                    last = pe.matmul(ps[0:QC, 1 + c // 4, 128 * (c % 4):128 * (c % 4) + 128],
                                     ablk[:, QC * c:QC * c + QC], wo[:, :], start=True, stop=True)
                last.then_inc(sA["z_done"], 1)

            def spread_rows(a, n):
                pe.wait_ge(sA["spread_ready"], NC * a + NC)
                pe.wait_ge(sA["z_parts"], 2 * a + 2)
                pe.wait_ge(sA["z_part2"], a + 1)
                for k in range(3):
                    for c in range(NC):
                        last = pe.matmul(ps[:, 2 + n, 0:LH], zpart[k][:, c, :], spread[:, c, LH * n:LH * n + LH],
                                         start=(k == 0 and c == 0), stop=(k == 2 and c == NC - 1))
                if n == 1:
                    last.then_inc(sA["spread_done"], 1)

            def center1(b):
                if later(6 * (b - 1)):
                    pe.wait_ge(sC["even_read"], 6 * (b - 1))
                    pe.wait_ge(sC["odd_read"], 6 * (b - 1))
                pe.wait_ge(sA["res_ready"], b + 1)
                if later(b):
                    pe.wait_ge(sB["pooled_ready"], b)
                for n in range(2):
                    last = pe.matmul(ps[:, 4 + n, 0:LH], center[:, :], res[:, n, :], start=True, stop=True)
                last.then_inc(sB["center1"], 1)

            def variance(b, k):
                pe.wait_ge(sB[f"cen{k}"], b + 1)
                pe.wait_ge(sB[f"squared{k}"], b + 1)
                for n in range(2):
                    last = pe.matmul(ps[:, 4 + n, 0:LH], mean[:, :], bsq[:, n, :], start=True, stop=True)
                last.then_inc(sB[f"var{k}"], 1)

            def widen(b, k):
                if k == 0:
                    pe.wait_ge(sB["hid1"], b + 1)
                else:
                    pe.wait_ge(sB["ff_act"], NF * b + k)
                    pe.wait_ge(sB["ff_dve"], NF * b + k)
                for n in range(2):
                    last = pe.matmul(ps[:, 4 + n, 0:LH], f1w[:, 128 * k:128 * k + 128], hid[:, n, :],
                                     start=True, stop=True)
                last.then_inc(sB["f1_done"], 1)

            def narrow(b, n):
                pe.wait_ge(sB["ff_act"], NF * b + NF)
                pe.wait_ge(sB["ff_dve"], NF * b + NF)
                pe.matmul(ps[:, 4 + n, 0:LH], center[:, :], hid[:, n, :], start=True, stop=False)
                for k in range(NF):
                    last = pe.matmul(ps[:, 4 + n, 0:LH], f2c[:, k, :], ff[:, k, n, :], start=False,
                                     stop=(k == NF - 1))
                if n == 1:
                    last.then_inc(sB["center2"], 1)

            def conv(b, n):
                pe.wait_ge(sB["fused_ready"], b + 1)
                a, m = ((0, LH + 1), (LH + 1, LH - 1))[n]
                for k in range(3):
                    last = pe.matmul(ps[:, 4 + n, 0:m], cw[:, k, :], fused[:, a + k:a + k + m],
                                     start=(k == 0), stop=(k == 2))
                last.then_inc(sB["conv_done"], 1)

            def product(bank, lhs, rhs, done=None, rows=128, start=True, stop=True):
                last = pe.matmul(ps[0:rows, bank, 0:T], lhs, rhs, start=start, stop=stop)
                if done:
                    last.then_inc(sC[done], 1)

            def c_center(c, k):
                if k == 0:
                    pe.wait_ge(sB["h_ready"], c + 1)
                    if later(6 * c):
                        pe.wait_ge(sC["even_read"], 6 * c)
                        pe.wait_ge(sC["odd_read"], 6 * c)
                    product(6, center[:, :], hb[:, :], "c_center")
                else:
                    pe.wait_ge(sC["hn_ready"], c + 1)
                    product(6, center[:, :], hn[:, :], "c_center")

            def c_variance(c, k):
                pe.wait_ge(sC["c_squared"], 3 * c + k + 1)
                product(7, mean[:, :], csq[:, :], "c_var")

            def project(c):
                pe.wait_ge(sC["xn_ready"], c + 1)
                product(6, w_in[:, 0:128], xn[:, :], "xs_done")
                product(7, w_in[:, 128:256], xn[:, :], "z_proj")

            def c_widen(a, c):
                if a is None:
                    pe.wait_ge(sA["ao_ready"], B)
                else:
                    pe.wait_ge(sA["v_ready"], a + 1)
                    pe.wait_ge(sA["mo_ready"], a + 1)
                for k in range(2):
                    product(2 + k, ffn1[:, 128 * k:128 * k + 128], xn[:, :], "g_done")

            def time_steps(c):
                pe.wait_ge(sC["xs_ready"], c + 1)
                pe.wait_ge(sC["sz_ready"], c + 1)
                product(6, w_dt[:, :], xs, "dt_done")
                product(7, w_bc[:, :], xs, "bc_done", rows=2 * DS)

            def gram(c):
                pe.wait_ge(sC["bt_ready"], c + 1)
                pe.wait_ge(sC["ct_ready"], c + 1)
                pe.wait_ge(sC["abs_ready"], c + 1)
                pe.wait_ge(sC["dt_max"], c + 1)
                for k, (bank, at) in enumerate(((6, 0), (7, 0), (7, T - LC))):
                    last = pe.matmul(ps[0:LC, bank, at:at + T - LC * k], bt[:, LC * k:LC * k + LC], ct[:, LC * k:T],
                                     start=True, stop=True)
                last.then_inc(sC["gram_done"], 1)

            def turn_scaled(c):
                pe.wait_ge(sC["gm_ready"], c + 1)
                pe.wait_ge(sC["scl_ready"], c + 1)
                for k in range(NT):
                    last = pe.transpose(ps[0:LC, 6, 128 * k:128 * k + 128], dtx[:, LC * k:LC * k + LC], ident[:, :])
                last.then_inc(sC["scl_turned"], 1)

            def scan_sum(c):
                pe.wait_ge(sC["sct_ready"], c + 1)
                for k in range(NT):
                    last = pe.matmul(ps[:, 7, LC * k:T], sct[:, k, :], gm[:, k, LC * k:T], start=(k == 0),
                                     stop=(k == NT - 1), skip_group_check=True)
                last.then_inc(sC["y_done"], 1)

            def block_out(c):
                for k in range(2):
                    product(6, tail[:, 1 + k, :], g[:, k, :], start=(k == 0), stop=False)
                pe.wait_ge(sC["y_ready"], c + 1)
                product(6, tail[:, 0, :], t1_y[:, :], "tail_done", start=False)

            def logits(c):
                pe.wait_ge(sC["xf_ready"], c + 1)
                pe.wait_ge(sC["c_rstd"], 3 * c + 3)
                for k in range(NT):
                    last = pe.matmul(ps[0:LC, 7, 384 + E * k:384 + E * k + E], xf[:, LC * k:LC * k + LC], sw_t[:, :],
                                     start=True, stop=True)
                last.then_inc(sC["logit_done"], 1)
                for k in range(NT):
                    last = pe.matmul(ps[0:LC, 6, 128 * k:128 * k + 128], xf[:, LC * k:LC * k + LC], ident[:, :],
                                     start=True, stop=True)
                last.then_inc(sC["own_done"], 1)

            def counts(c):
                pe.wait_ge(sC["oh_ready"], c + 1)
                for k in range(NT + 1):
                    for m in range(min(k + 1, NT)):
                        last = pe.matmul(ps[0:LC, 7, 384 + E * k:384 + E * k + E],
                                         (causal16 if m == k else ones16)[:, :], oh16[:, m, :],
                                         start=(m == 0), stop=(m == min(k, NT - 1)))
                last.then_inc(sC["cnt_done"], 1)

            def turn_weights(c):
                pe.wait_ge(sC["wgt_ready"], c + 1)
                for k in range(NT):
                    last = pe.transpose(ps[0:E, 7, LC * k:LC * k + LC], wgt[:, k, :], ident[0:LC, 0:LC])
                last.then_inc(sC["wt_done"], 1)

            def own_rows(c):
                pe.wait_ge(sC["wt_ready"], c + 1)
                for k in range(NT):
                    at = slice(LC * k, LC * k + LC)
                    pe.matmul(ps[0:LC, 7, 128 * k:128 * k + 128], hn[:, at], ident[:, :], start=True, stop=False)
                    last = pe.matmul(ps[0:LC, 7, 128 * k:128 * k + 128], wt[:, at], eb[:, :], start=False, stop=True)
                last.then_inc(sC["base_done"], 1)

            def experts(b, c, k):
                for n in range(4):
                    if k == 0 and n == 0:
                        pe.wait_ge(sB["pooled_ready"], B if b is None else b + 1)
                    elif k == 0 and n == 2:
                        pe.wait_ge(sC["own_ready"], c + 1)
                    elif k == 0 and n == 3:
                        pe.wait_ge(sC["base_ready"], c + 1)
                    elif k > 0 and n % 2 == 0:
                        pe.wait_ge(sC["even_read"], 6 * c + 2 * k - 1 + n // 2)
                    elif k > 0:
                        pe.wait_ge(sC["odd_read"], 6 * c + 2 * k - 1 + n // 2)
                    pe.matmul(ps[0:LC, 4 + n, :], xf[:, LC * k:LC * k + LC], ew_t[:, 512 * n:512 * n + 512],
                              start=True, stop=True).then_inc(sC["exp_done"], 1)

            def turn(a, b, c, more=True):
                A, Bb, C = a is not None, b is not None, c is not None
                if C: c_center(c, 0)
                if Bb: center1(b)
                if A: keys(a)
                if C: c_variance(c, 0)
                if A: queries_values(a)
                if C: c_variance(c, 1)
                if A: mean_out(a)
                if C: project(c)
                if C: c_widen(a, c)
                if Bb: variance(b, 1)
                if A: gather(a)
                if A: scores(a, 0)
                if C: time_steps(c)
                if A: scores(a, 1)
                if Bb: widen(b, 0)
                if A: turn_probs(a, 0)
                if A: scores(a, 2); turn_probs(a, 1)
                if Bb: widen(b, 1)
                if A: scores(a, 3); turn_probs(a, 2)
                if C: gram(c)
                if A: scores(a, 4); turn_probs(a, 3)
                if Bb: widen(b, 2)
                if A: scores(a, 5); turn_probs(a, 4)
                if C: turn_scaled(c)
                if A: scores(a, 6); turn_probs(a, 5)
                if Bb: widen(b, 3)
                if C: scan_sum(c)
                if A: scores(a, 7); turn_probs(a, 6)
                if Bb: narrow(b, 0)
                if C: block_out(c)
                if A: scores(a, 8); turn_probs(a, 7)
                if Bb: narrow(b, 1)
                if C: c_center(c, 1)
                if A: scores(a, 9); turn_probs(a, 8)
                if Bb: variance(b, 2)
                if C: c_variance(c, 2)
                if A: turn_probs(a, 9)
                if C: logits(c)
                if A: attend(a)
                if C: counts(c)
                if A: attend_out(a)
                if Bb: conv(b, 0)
                if C: turn_weights(c)
                if Bb: conv(b, 1)
                if C: own_rows(c)
                if C: experts(b, c, 0)
                if A: spread_rows(a, 0)
                if A: spread_rows(a, 1)
                if A and more: turn_x(a + 1)
                if C: experts(b, c, 1)
                if C: experts(b, c, 2)

            turn_x(0)
            turns(turn, pe)

        @block.scalar
        def _(act):
            act.wait_ge(sA["zeroed"], 4)
            A_SETS = "natural_log_exp_and_others", "gelu_and_others"

            def copy_x(a):
                act.wait_ge(sA["x_turned"], a + 1)
                if later(a):
                    act.wait_ge(sA["x_kept"], a)
                act.activation(xt[:, :, :], ps[:, 0:2, 0:LH], ACT.Copy).then_inc(sA["xt_ready"], 1)

            def copy_keys(a):
                act.wait_ge(sA["k_done"], a + 1)
                act.activation(kt[:, :, :], ps[:, 2:4, 0:LH], ACT.Identity, bias=col("k_b")).then_inc(sA["kt_ready"], 1)

            def copy_queries(a):
                act.wait_ge(sA["qv_done"], a + 1)
                act.activation(qtok[:, :, :].rearrange("p (b c) d -> p b c d", b=3),
                               ps[0:LC, 0:3, :].rearrange("p b (c n) -> p b c n", c=2)[:, :, :, 0:128],
                               ACT.Copy).then_inc(sA["q_ready"], 1)

            def exps(a, c):
                act.wait_ge(sA["max_ready"], NC * a + c + 1)
                if c >= 2:
                    act.wait_ge(sA["prob_turned"], NC * a + c - 1)
                act.activation(prob[:, c % 2, :].rearrange("p (n l) -> p n l", n=2), ps[0:QC, 0:2, 0:LH],
                               ACT.Exp, bias=nmax[:, c:c + 1], accum_out=den[:, c:c + 1])\
                   .then_inc(sA["prob_ready"], 1)

            def copy_probs(a, c):
                act.wait_ge(sA["prob_turned"], NC * a + c + 1)
                act.activation(probt[:, 3:6, QC * c:QC * c + QC],
                               ps[0:LC, 3, 0:3 * QC].rearrange("p (c q) -> p c q", c=3), ACT.Copy)\
                   .then_inc(sA["probt_act"], 1)

            def z_high(a):
                act.wait_ge(sA["z_ready"], a + 1)
                act.activation(zpart[0][:, :, :], z[:, :, :], ACT.Copy).then_inc(sA["z_parts"], 1)

            def z_middle(a):
                act.wait_ge(sA["z_res"], a + 1)
                act.activation(zpart[1][:, :, :], z[:, :, :], ACT.Copy).then_inc(sA["z_parts"], 1)

            def attention_out(a):
                act.wait_ge(sA["spread_done"], a + 1)
                if later(a):
                    act.wait_ge(sB["fused_ready"], a)
                act.activation(ao[:, :, :], ps[:, 2:4, 0:LH], ACT.Identity, bias=mo[:, 0:1]).then_inc(sA["ao_ready"], 1)

            def squares(b, k):
                act.wait_ge(sB[f"center{k}"], b + 1)
                bias = {} if k == 1 else {"bias": f2_bc[:, 0:1]}
                act.activation(bsq[:, :, :], ps[:, 4:6, 0:LH], ACT.Square, **bias).then_inc(sB[f"squared{k}"], 1)
                act.activation(cen[:, :, :], ps[:, 4:6, 0:LH], ACT.Identity, **bias).then_inc(sB[f"cen{k}"], 1)

            def deviation(b, k, steps):
                act.wait_ge(sB[f"var{k}"], b + 1)
                act.activation(bsq[:, :, :], ps[:, 4:6, 0:LH], ACT.Ln, bias=eps5[:, 0:1])\
                   .then_inc(sB["b_act"], 1)
                act.wait_ge(sB["b_act"], steps.next())
                act.activation(bsq[:, :, :], bsq[:, :, :], ACT.Exp, scale=-0.5).then_inc(sB[f"rstd{k}"], 1)

            def rectify(b, k):
                act.wait_ge(sB["f1_done"], NF * b + k + 1)
                if k == 0 and later(NT * (b - 1)):
                    act.wait_ge(sC["rows_ready"], NT * (b - 1))
                act.activation(ff[:, k, 0], ps[:, 4, 0:LH], ACT.Relu, bias=vec[:, F1B + k:F1B + k + 1])\
                   .then_inc(sB["ff_act"], 1)

            def pool_out(b):
                act.wait_ge(sB["pooled_ready"], b + 1)
                if later(b):
                    act.wait_ge(sC["hn_ready"], b)
                act.activation(hb[:, :], pooled[:, :], ACT.Relu, bias=col("conv_b")).then_inc(sB["h_ready"], 1)

            def c_square(c, k):
                if k == 1:
                    act.wait_ge(sC["u_ready"], c + 1)
                    act.activation(csq[:, :], u[:, :], ACT.Square).then_inc(sC["c_squared"], 1)
                else:
                    act.wait_ge(sC["c_center"], 2 * c + 1 + k // 2)
                    act.activation(csq[:, :], ps[:, 6, 0:T], ACT.Square).then_inc(sC["c_squared"], 1)

            def c_deviation(c, k, steps):
                act.wait_ge(sC["c_var"], 3 * c + k + 1)
                act.activation(csq[:, :], ps[:, 7, 0:T], ACT.Ln, bias=(eps6 if k == 1 else eps5)[:, 0:1])\
                   .then_inc(sC["c_act"], 1)
                act.wait_ge(sC["c_act"], steps.next())
                act.activation(csq[:, :], csq[:, :], ACT.Exp, scale=-0.5).then_inc(sC["c_rstd"], 1)

            def gates(c):
                act.wait_ge(sC["xs_done"], c + 1)
                act.activation(xp[:, 3:T + 3], ps[:, 6, 0:T], ACT.Copy).then_inc(sC["xp_ready"], 1)
                act.preload_act_table_set("gelu_and_others")
                for k in range(2):
                    act.wait_ge(sC["g_done"], 2 * c + k + 1)
                    act.activation(g[:, k, :], ps[:, 2 + k, 0:T], ACT.Gelu).then_inc(sC["g_ready"], 1)
                act.wait_ge(sC["z_proj"], c + 1)
                act.activation(sz, ps[:, 7, 0:T], ACT.Tanh, scale=0.5).then_inc(sC["th_z"], 1)
                act.wait_ge(sC["c_ready"], c + 1)
                act.activation(xs, c_[:, :], ACT.Tanh, scale=0.5).then_inc(sC["th_c"], 1)
                act.preload_act_table_set("natural_log_exp_and_others")

            def softplus(c):
                act.wait_ge(sC["dt_done"], c + 1)
                act.activation(ee_ep[:, :], ps[:, 6, 0:T], ACT.Abs, bias=col("b_dt")).then_inc(sC["abs_ready"], 1)
                act.wait_ge(sC["abs_ready"], c + 1)
                act.activation(ee_ep[:, :], ee_ep[:, :], ACT.Exp, scale=-1.0).then_inc(sC["e_ready"], 1)
                act.wait_ge(sC["bc_done"], c + 1)
                act.activation(bt[:, :], ps[0:DS, 7, 0:T], ACT.Copy).then_inc(sC["bt_ready"], 1)
                act.activation(ct[:, :], ps[DS:2 * DS, 7, 0:T], ACT.Copy).then_inc(sC["ct_ready"], 1)

            def logarithm(c):
                act.wait_ge(sC["w1_ready"], c + 1)
                act.activation(lw_la[:, :], w1_cum[:, :], ACT.Ln).then_inc(sC["lw_ready"], 1)

            def decays(c):
                act.wait_ge(sC["cum_ready"], c + 1)
                act.activation(t2_en[:, :], w1_cum[:, :], ACT.Exp, scale=-1.0).then_inc(sC["en_ready"], 1)
                act.activation(ee_ep[:, :], w1_cum[:, :], ACT.Exp).then_inc(sC["ep_ready"], 1)

            def copy_scaled(c):
                act.wait_ge(sC["scl_turned"], c + 1)
                act.activation(sct[:, :, :], ps[0:LC, 6, 0:384].rearrange("p (c d) -> p c d", c=NT), ACT.Copy)\
                   .then_inc(sC["sct_ready"], 1)

            def route_exp(c):
                act.wait_ge(sC["lg_ready"], c + 1)
                act.activation(ex[:, :, :], lg[:, :, :], ACT.Exp).then_inc(sC["ex_ready"], 1)

            def copy_weights(c):
                act.wait_ge(sC["wt_done"], c + 1)
                act.activation(wt[:, :], ps[0:E, 7, 0:T], ACT.Copy).then_inc(sC["wt_ready"], 1)

            def experts(b, c, k):
                act.wait_ge(sC["wgt_ready"], c + 1)
                act.wait_ge(sB["center2"], B if b is None else b + 1)
                if b is None and k == 0:
                    act.wait_ge(sC["rows_ready"], NT * c)
                if k == 2:
                    act.wait_ge(sC["rows_ready"], NT * c + 1)
                for n in range(2):
                    act.wait_ge(sC["exp_done"], 12 * c + 4 * k + 2 * n + 2)
                    for j in range(4):
                        e = 8 * n + 4 + j
                        last = act.activation(part_rows[:, k % 2, 4 * n + j, :], ps[0:LC, 5 + 2 * n, 128 * j:128 * j + 128],
                                              ACT.Copy, scale=wgt[:, k, e:e + 1])
                    last.then_inc(sC["odd_read"], 1)

            def copy_base(c):
                act.wait_ge(sC["base_done"], c + 1)
                act.activation(base[:, :, :], ps[0:LC, 7, 0:384].rearrange("p (c d) -> p c d", c=NT), ACT.Copy)\
                   .then_inc(sC["base_ready"], 1)

            def turn(a, b, c, more=True):
                A, Bb, C = a is not None, b is not None, c is not None
                act.preload_act_table_set("natural_log_exp_and_others")
                bsteps = Steps(b, 2) if Bb else None
                csteps = Steps(c, 3) if C else None
                if C: c_square(c, 0)
                if Bb: squares(b, 1)
                if A: copy_keys(a)
                if C: c_deviation(c, 0, csteps)
                if C: c_square(c, 1)
                if A: copy_queries(a)
                if C: c_deviation(c, 1, csteps)
                if C: gates(c)
                if Bb: deviation(b, 1, bsteps)
                if A: exps(a, 0)
                if C: softplus(c)
                if A: exps(a, 1); copy_probs(a, 0)
                if Bb: rectify(b, 0)
                if C: logarithm(c)
                if A: exps(a, 2); copy_probs(a, 1)
                if Bb: rectify(b, 1)
                if A: exps(a, 3); copy_probs(a, 2)
                if C: decays(c)
                if A: exps(a, 4); copy_probs(a, 3)
                if Bb: rectify(b, 2)
                if A: exps(a, 5); copy_probs(a, 4)
                if C: copy_scaled(c)
                if A: exps(a, 6); copy_probs(a, 5)
                if Bb: rectify(b, 3)
                if A: exps(a, 7); copy_probs(a, 6)
                if A: exps(a, 8)
                if Bb: squares(b, 2)
                if A: copy_probs(a, 7)
                if C: c_square(c, 2)
                if A: exps(a, 9); copy_probs(a, 8)
                if C: c_deviation(c, 2, csteps)
                if A: copy_probs(a, 9)
                if Bb: deviation(b, 2, bsteps)
                if C: route_exp(c)
                if C: copy_weights(c)
                if A: z_high(a)
                if A: z_middle(a)
                if C: copy_base(c)
                if Bb: pool_out(b)
                if C: experts(b, c, 0)
                if A: attention_out(a)
                if A and more: copy_x(a + 1)
                if C: experts(b, c, 1)
                if C: experts(b, c, 2)
                for steps in (bsteps, csteps):
                    if steps:
                        steps.end()

            copy_x(0)
            turns(turn, act)

        @block.vector
        def _(dve):
            dve.wait_ge(sA["zeroed"], 4)

            def copy_places(a):
                if later(NL * a):
                    dve.wait_ge(sA["pick_ready"], NL * a)
                dve.tensor_copy(place[:, :, :], place_t[:, :, bass.ds(H * a, H)]).then_inc(sA["place_ready"], 1)

            def take_mean(a, steps):
                dve.wait_ge(sA["xt_ready"], a + 1)
                dve.tensor_reduce(xmean[:, :], xt[:, :, :], AX.XY, ALU.add).then_inc(sA["a_dve"], 1)
                dve.wait_ge(sA["a_dve"], steps.next())
                dve.tensor_scalar(xmean[:, :], xmean[:, :], 1.0 / L, None, ALU.mult).then_inc(sA["a_dve"], 1)
                dve.wait_ge(sA["a_dve"], steps.next())
                dve.tensor_scalar(xc[:, :, :], xt[:, :, :], xmean[:, 0:1], None, ALU.subtract)\
                   .then_inc(sA["mean_ready"], 1)

            def copy_values(a):
                dve.wait_ge(sA["q_ready"], a + 1)
                dve.tensor_copy(vtok[:, :, :].rearrange("p (b c) d -> p b c d", b=3),
                                ps[0:LC, 0:3, :].rearrange("p b (c n) -> p b c n", c=2)[:, :, :, 128:256])\
                   .then_inc(sA["v_ready"], 1)

            def means(a):
                dve.wait_ge(sA["means_done"], a + 1)
                dve.tensor_scalar(mv[:, :], ps[:, 3, 1:2], col("v_b"), None, ALU.add).then_inc(sA["mv_ready"], 1)
                dve.tensor_scalar(qb[:, :], ps[:, 3, 0:1], col("q_b"), None, ALU.add).then_inc(sA["qb_ready"], 1)
                dve.wait_ge(sA["mo_done"], a + 1)
                dve.tensor_scalar(mo[:, :], ps[:, 3, 2:3], col("o_b"), None, ALU.add).then_inc(sA["mo_ready"], 1)

            def block_queries(a):
                dve.wait_ge(sA["gathered"], a + 1)
                dve.wait_ge(sA["qb_ready"], a + 1)
                for j in range(4):
                    p = slice(32 * j, 32 * j + 32)
                    last = dve.scalar_tensor_tensor(out=blk[p, PQ * j:PQ * j + PQ], in0=ps[p, 0, 0:PQ],
                                                    scalar=qb[p, 0:1], in1=pair_scale[p, :],
                                                    op0=ALU.add, op1=ALU.mult)
                last.then_inc(sA["blk_ready"], 1)

            def row_max(a, c):
                dve.wait_ge(sA["scored"], NC * a + c + 1)
                dve.tensor_reduce(nmax[:, c:c + 1], ps[0:QC, 0:2, 0:LH], AX.XY, ALU.max, negate=True)\
                   .then_inc(sA["max_ready"], 1)

            def copy_probs(a, c):
                dve.wait_ge(sA["prob_turned"], NC * a + c + 1)
                dve.tensor_copy(probt[:, 0:3, QC * c:QC * c + QC],
                                ps[0:LC, 2, 0:3 * QC].rearrange("p (c q) -> p c q", c=3))\
                   .then_inc(sA["probt_dve"], 1)

            def spread_chunk(a, c):
                if c == 0:
                    dve.wait_ge(sA["place_loaded"], 16 * len(runs) * (a + 1))
                dve.tensor_scalar(spread[:, c, :], spread[:, c, :], place_of[0:QC, c:c + 1], None,
                                  ALU.is_equal).then_inc(sA["spread_ready"], 1)

            def block_rows(a, steps):
                dve.wait_ge(sA["prob_ready"], NC * a + NC)
                dve.reciprocal(rden[:, :], den[:, :]).then_inc(sA["a_dve"], 1)
                dve.wait_ge(sA["a_dve"], steps.next())
                dve.wait_ge(sA["av_done"], a + 1)
                for j in range(4):
                    p = slice(32 * j, 32 * j + 32)
                    last = dve.tensor_tensor(ablk[p, PQ * j:PQ * j + PQ], ps[p, 0, 0:PQ], pair_mask[p, :], ALU.mult)
                last.then_inc(sA["ablk_ready"], 1)

            def z_rows(a):
                dve.wait_ge(sA["z_done"], a + 1)
                rows = ps[0:QC, 1:4, :].rearrange("p b n -> p (b n)")[:, 0:NC * 128].rearrange("p (c n) -> p c n", c=NC)
                dve.tensor_tensor(z[:, :, :], rows, rden[:, :, None].broadcast_to([QC, NC, 128]), ALU.mult)\
                   .then_inc(sA["z_ready"], 1)

            def z_rest(a):
                dve.wait_ge(sA["z_parts"], 2 * a + 1)
                dve.tensor_tensor(z[:, :, :], z[:, :, :], zpart[0][:, :, :], ALU.subtract).then_inc(sA["z_res"], 1)

            def z_low(a):
                dve.wait_ge(sA["z_parts"], 2 * a + 2)
                dve.tensor_tensor(zpart[2][:, :, :], z[:, :, :], zpart[1][:, :, :], ALU.subtract)\
                   .then_inc(sA["z_part2"], 1)

            def residual(a):
                dve.wait_ge(sA["ao_ready"], a + 1)
                dve.wait_ge(sA["x_kept"], a + 1)
                dve.tensor_tensor(res[:, :, :], res[:, :, :], ao[:, :, :], ALU.add).then_inc(sA["res_ready"], 1)

            def normed(b, k, scale, bias, steps):
                dve.wait_ge(sB[f"rstd{k}"], b + 1)
                if k == 2:
                    dve.wait_ge(sB["center2"], b + 1)
                dve.tensor_tensor(hid[:, :, :], cen[:, :, :], bsq[:, :, :], ALU.mult)\
                   .then_inc(sB["b_dve"], 1)
                dve.wait_ge(sB["b_dve"], steps.next())
                dve.tensor_scalar(hid[:, :, :], hid[:, :, :], col(scale), col(bias), ALU.mult, ALU.add)\
                   .then_inc(sB[f"hid{k}"], 1)

            def rectify(b, k):
                dve.wait_ge(sB["f1_done"], NF * b + k + 1)
                if k == 0 and later(NT * (b - 1)):
                    dve.wait_ge(sC["rows_ready"], NT * (b - 1))
                dve.tensor_scalar(ff[:, k, 1], ps[:, 5, 0:LH], vec[:, F1B + k:F1B + k + 1], 0.0,
                                  ALU.add, ALU.max).then_inc(sB["ff_dve"], 1)

            def fuse(b):
                dve.wait_ge(sB["hid2"], b + 1)
                dve.tensor_tensor(fused[:, 1:L + 1].rearrange("p (n l) -> p n l", n=2), hid[:, :, :], ao[:, :, :],
                                  ALU.add).then_inc(sB["fused_ready"], 1)

            def pool_half(b, n, steps):
                dve.wait_ge(sB["conv_done"], 2 * b + n + 1)
                m = (LH + 1) // 2
                at, w = ((0, m), (m, T - m))[n]
                ins = dve.tensor_reduce(pooled[:, at:at + w],
                                        ps[:, 4 + n, 0:2 * w].rearrange("p (t two) -> p t two", two=2),
                                        AX.X, ALU.max)
                if n == 0:
                    ins.then_inc(sB["b_dve"], 1)
                    dve.wait_ge(sB["b_dve"], steps.next())
                else:
                    ins.then_inc(sB["pooled_ready"], 1)

            def c_normed(c):
                dve.wait_ge(sC["c_rstd"], 3 * c + 1)
                dve.tensor_tensor(u[:, :], ps[:, 6, 0:T], csq[:, :], ALU.mult).then_inc(sC["u_ready"], 1)

            def c_normed2(c):
                dve.wait_ge(sC["c_rstd"], 3 * c + 2)
                dve.scalar_tensor_tensor(out=xn[:, :], in0=u[:, :], scalar=col("norm_w"), in1=csq[:, :],
                                         op0=ALU.mult, op1=ALU.mult).then_inc(sC["xn_ready"], 1)

            def depthwise(c, steps):
                dve.wait_ge(sC["xp_ready"], c + 1)
                dve.tensor_scalar(c_[:, :], xp[:, 0:T], vec[:, ACW:ACW + 1], col("aconv_b"), ALU.mult, ALU.add)\
                   .then_inc(sC["c_dve"], 1)
                dve.wait_ge(sC["c_dve"], steps.next())
                for k in (1, 2, 3):
                    ins = dve.scalar_tensor_tensor(out=c_[:, :], in0=xp[:, k:k + T], scalar=vec[:, ACW + k:ACW + k + 1],
                                                   in1=c_[:, :], op0=ALU.mult, op1=ALU.add)
                    if k < 3:
                        ins.then_inc(sC["c_dve"], 1)
                        dve.wait_ge(sC["c_dve"], steps.next())
                    else:
                        ins.then_inc(sC["c_ready"], 1)

            def silus(c, steps):
                dve.wait_ge(sC["th_z"], c + 1)
                dve.tensor_scalar(sz, sz, 0.5, 0.5, ALU.mult, ALU.add).then_inc(sC["c_dve"], 1)
                dve.wait_ge(sC["c_dve"], steps.next())
                dve.tensor_tensor(sz, sz, ps[:, 7, 0:T], ALU.mult).then_inc(sC["sz_ready"], 1)
                dve.wait_ge(sC["th_c"], c + 1)
                dve.tensor_scalar(xs, xs, 0.5, 0.5, ALU.mult, ALU.add).then_inc(sC["c_dve"], 1)
                dve.wait_ge(sC["c_dve"], steps.next())
                dve.tensor_tensor(xs, xs, c_[:, :], ALU.mult).then_inc(sC["xs_ready"], 1)

            def softplus(c, steps):
                dve.wait_ge(sC["abs_ready"], c + 1)
                dve.tensor_scalar(dt[:, :], ps[:, 6, 0:T], col("b_dt"), 0.0, ALU.add, ALU.max).then_inc(sC["dt_max"], 1)
                dve.wait_ge(sC["e_ready"], c + 1)
                dve.scalar_tensor_tensor(out=t1_y[:, :], in0=ee_ep[:, :], scalar=SMALL_E, in1=ee_ep[:, :],
                                         op0=ALU.is_ge, op1=ALU.mult).then_inc(sC["c_dve"], 1)
                dve.wait_ge(sC["c_dve"], steps.next())
                dve.tensor_scalar(w1_cum[:, :], t1_y[:, :], 1.0, None, ALU.add).then_inc(sC["w1_ready"], 1)

            def softplus2(c, steps):
                dve.tensor_scalar(t2_en[:, :], ee_ep[:, :], 1.0 / 3, -0.5, ALU.mult, ALU.add)\
                   .then_inc(sC["c_dve"], 1)
                dve.wait_ge(sC["c_dve"], steps.next())
                dve.tensor_tensor(t2_en[:, :], t2_en[:, :], ee_ep[:, :], ALU.mult).then_inc(sC["c_dve"], 1)
                dve.wait_ge(sC["c_dve"], steps.next())
                dve.wait_ge(sC["w1_ready"], c + 1)
                dve.scalar_tensor_tensor(out=t1_y[:, :], in0=w1_cum[:, :], scalar=-1.0, in1=ee_ep[:, :],
                                         op0=ALU.add, op1=ALU.subtract).then_inc(sC["c_dve"], 1)
                dve.wait_ge(sC["c_dve"], steps.next())
                dve.scalar_tensor_tensor(out=t1_y[:, :], in0=t2_en[:, :], scalar=1.0, in1=t1_y[:, :],
                                         op0=ALU.add, op1=ALU.mult).then_inc(sC["c_dve"], 1)
                dve.wait_ge(sC["c_dve"], steps.next())
                dve.wait_ge(sC["dt_max"], c + 1)
                dve.tensor_tensor(dt[:, :], dt[:, :], t1_y[:, :], ALU.subtract).then_inc(sC["c_dve"], 1)
                dve.wait_ge(sC["c_dve"], steps.next())

            def decays(c, steps):
                dve.wait_ge(sC["lw_ready"], c + 1)
                dve.scalar_tensor_tensor(out=lw_la[:, :], in0=w1_cum[:, :], scalar=1.0, in1=lw_la[:, :],
                                         op0=ALU.is_gt, op1=ALU.mult).then_inc(sC["c_dve"], 1)
                dve.wait_ge(sC["c_dve"], steps.next())
                dve.tensor_tensor(dt[:, :], dt[:, :], lw_la[:, :], ALU.add).then_inc(sC["c_dve"], 1)
                dve.wait_ge(sC["c_dve"], steps.next())
                dve.tensor_scalar(lw_la[:, :], dt[:, :], neg_a[:, 0:1], -20.0, ALU.mult, ALU.max)\
                   .then_inc(sC["c_dve"], 1)
                dve.wait_ge(sC["c_dve"], steps.next())
                dve.tensor_scalar(lw_la[:, :], lw_la[:, :], 20.0, None, ALU.min).then_inc(sC["c_dve"], 1)
                dve.wait_ge(sC["c_dve"], steps.next())

            def decays2(c, steps):
                dve.tensor_tensor_scan(w1_cum[:, :], ones[:, 0:1].broadcast_to([128, T]), lw_la[:, :], 0.0, ALU.mult, ALU.add)\
                   .then_inc(sC["cum_ready"], 1)
                dve.tensor_tensor(dtx[:, :], dt[:, :], xs, ALU.mult).then_inc(sC["c_dve"], 1)
                dve.wait_ge(sC["c_dve"], steps.next())

            def mask_gram(c):
                dve.wait_ge(sC["gram_done"], c + 1)
                for k, (bank, at) in enumerate(((6, 0), (7, 0), (7, T - LC))):
                    n = T - LC * k
                    last = dve.tensor_tensor(gm[:, k, LC * k:T], ps[0:LC, bank, at:at + n], causal[:, 0:n], ALU.mult)
                last.then_inc(sC["gm_ready"], 1)

            def scaled(c):
                dve.wait_ge(sC["en_ready"], c + 1)
                dve.tensor_tensor(dtx[:, :], dtx[:, :], t2_en[:, :], ALU.mult).then_inc(sC["scl_ready"], 1)

            def scan_out(c, steps):
                dve.wait_ge(sC["ep_ready"], c + 1)
                dve.wait_ge(sC["y_done"], c + 1)
                dve.tensor_tensor(t1_y[:, :], ee_ep[:, :], ps[:, 7, 0:T], ALU.mult).then_inc(sC["c_dve"], 1)
                dve.wait_ge(sC["c_dve"], steps.next())
                dve.scalar_tensor_tensor(out=t1_y[:, :], in0=xs, scalar=col("D_param"), in1=t1_y[:, :],
                                         op0=ALU.mult, op1=ALU.add).then_inc(sC["c_dve"], 1)
                dve.wait_ge(sC["c_dve"], steps.next())
                dve.tensor_tensor(t1_y[:, :], t1_y[:, :], sz, ALU.mult).then_inc(sC["y_ready"], 1)

            def block_out(c, steps):
                dve.wait_ge(sC["tail_done"], c + 1)
                dve.tensor_tensor(hn[:, :], ps[:, 6, 0:T], u[:, :], ALU.add).then_inc(sC["c_dve"], 1)
                dve.wait_ge(sC["c_dve"], steps.next())
                dve.tensor_tensor(hn[:, :], hn[:, :], hb[:, :], ALU.add).then_inc(sC["hn_ready"], 1)

            def c_normed3(c):
                dve.wait_ge(sC["c_rstd"], 3 * c + 3)
                dve.tensor_tensor(xf[:, :], ps[:, 6, 0:T], csq[:, :], ALU.mult).then_inc(sC["xf_ready"], 1)

            def by_expert(column):
                return column.broadcast_to([LC, NT, E])

            negmax, total, inv, top, p_top, pos, kept, passed = (m3[:, k, :] for k in range(8))

            def route(c, steps):
                dve.wait_ge(sC["logit_done"], c + 1)
                dve.tensor_tensor(lg[:, :, :], ps[0:LC, 7, 384:384 + NT * E].rearrange("p (c e) -> p c e", c=NT),
                                  by_expert(sb_row[0:LC, None, :]), ALU.add).then_inc(sC["c_dve"], 1)
                dve.wait_ge(sC["c_dve"], steps.next())
                dve.tensor_reduce(negmax, lg[:, :, :], AX.X, ALU.max, negate=True).then_inc(sC["c_dve"], 1)
                dve.wait_ge(sC["c_dve"], steps.next())
                dve.tensor_tensor(lg[:, :, :], lg[:, :, :], by_expert(m3[:, 0, :, None]), ALU.add)\
                   .then_inc(sC["lg_ready"], 1)

            def route2(c, steps):
                dve.wait_ge(sC["ex_ready"], c + 1)
                dve.tensor_reduce(top, ex[:, :, :], AX.X, ALU.max).then_inc(sC["c_dve"], 1)
                dve.wait_ge(sC["c_dve"], steps.next())
                dve.tensor_tensor(key[:, :, :], ex[:, :, :], by_expert(m3[:, 3, :, None]), ALU.is_equal)\
                   .then_inc(sC["c_dve"], 1)
                dve.wait_ge(sC["c_dve"], steps.next())
                dve.tensor_tensor(key[:, :, :], key[:, :, :], by_expert(tiebreak[:, None, :]), ALU.mult)\
                   .then_inc(sC["c_dve"], 1)
                dve.wait_ge(sC["c_dve"], steps.next())
                dve.tensor_reduce(pos, key[:, :, :], AX.X, ALU.max).then_inc(sC["c_dve"], 1)
                dve.wait_ge(sC["c_dve"], steps.next())
                dve.tensor_tensor(oh[:, :, :], key[:, :, :], by_expert(m3[:, 5, :, None]), ALU.is_equal)\
                   .then_inc(sC["c_dve"], 1)
                dve.wait_ge(sC["c_dve"], steps.next())
                dve.tensor_copy(oh16[:, :, :], oh[:, :, :]).then_inc(sC["oh_ready"], 1)
                dve.tensor_reduce(total, ex[:, :, :], AX.X, ALU.add).then_inc(sC["c_dve"], 1)
                dve.wait_ge(sC["c_dve"], steps.next())
                dve.reciprocal(inv, total).then_inc(sC["c_dve"], 1)
                dve.wait_ge(sC["c_dve"], steps.next())
                dve.tensor_tensor(p_top, top, inv, ALU.mult).then_inc(sC["c_dve"], 1)
                dve.wait_ge(sC["c_dve"], steps.next())

            def queue(c, steps):
                dve.wait_ge(sC["cnt_done"], c + 1)
                dve.tensor_tensor(cnt[:, :, :], ps[0:LC, 7, 384:384 + NT * E].rearrange("p (c e) -> p c e", c=NT),
                                  by_expert(run[:, None, :]), ALU.add).then_inc(sC["c_dve"], 1)
                dve.wait_ge(sC["c_dve"], steps.next())
                dve.tensor_tensor(run[:, :], run[:, :], ps[0:LC, 7, 384 + NT * E:384 + NT * E + E], ALU.add)\
                   .then_inc(sC["c_dve"], 1)
                dve.wait_ge(sC["c_dve"], steps.next())
                dve.tensor_tensor(cnt[:, :, :], cnt[:, :, :], oh[:, :, :], ALU.mult).then_inc(sC["c_dve"], 1)
                dve.wait_ge(sC["c_dve"], steps.next())
                dve.tensor_reduce(pos, cnt[:, :, :], AX.X, ALU.add).then_inc(sC["c_dve"], 1)
                dve.wait_ge(sC["c_dve"], steps.next())
                dve.tensor_scalar(kept, pos, float(CAP), None, ALU.is_le).then_inc(sC["c_dve"], 1)
                dve.wait_ge(sC["c_dve"], steps.next())
                dve.tensor_tensor(kept, kept, p_top, ALU.mult).then_inc(sC["c_dve"], 1)
                dve.wait_ge(sC["c_dve"], steps.next())
                dve.tensor_tensor(wgt[:, :, :], oh[:, :, :], by_expert(m3[:, 6, :, None]), ALU.mult)\
                   .then_inc(sC["wgt_ready"], 1)
                dve.tensor_tensor(passed, p_top, kept, ALU.subtract).then_inc(sC["c_dve"], 1)
                dve.wait_ge(sC["c_dve"], steps.next())

            def own_rows(c, steps):
                dve.wait_ge(sC["own_done"], c + 1)
                if later(16 * c):
                    dve.wait_ge(sC["stored"], 16 * c)
                for k in range(NT):
                    ins = dve.tensor_scalar(acc[:, k, :], ps[0:LC, 6, 128 * k:128 * k + 128], passed[:, k:k + 1], None,
                                            ALU.mult)
                ins.then_inc(sC["own_ready"], 1)

            def base_rows(c, steps):
                dve.wait_ge(sC["own_ready"], c + 1)
                dve.wait_ge(sC["base_ready"], c + 1)
                dve.tensor_tensor(acc[:, :, :], acc[:, :, :], base[:, :, :], ALU.add)\
                   .then_inc(sC["c_dve"], 1)
                dve.wait_ge(sC["c_dve"], steps.next())
                dve.wait_ge(sC["wgt_ready"], c + 1)

            def experts(c, k, steps):
                for n in range(2):
                    dve.wait_ge(sC["exp_done"], 12 * c + 4 * k + 2 * n + 1)
                    for j in range(4):
                        e = 8 * n + j
                        ins = dve.scalar_tensor_tensor(out=acc[:, k, :], in0=ps[0:LC, 4 + 2 * n, 128 * j:128 * j + 128],
                                                       scalar=wgt[:, k, e:e + 1], in1=acc[:, k, :],
                                                       op0=ALU.mult, op1=ALU.add)
                        if j < 3:
                            ins.then_inc(sC["c_dve"], 1)
                            dve.wait_ge(sC["c_dve"], steps.next())
                        else:
                            ins.then_inc(sC["even_read"], 1)
                            dve.wait_ge(sC["even_read"], 6 * c + 2 * k + n + 1)
                dve.sem_inc(sC["acc_ready"], 1)

            def turn(a, b, c, more=True):
                A, Bb, C = a is not None, b is not None, c is not None
                bsteps = Steps(b, 3) if Bb else None
                csteps = Steps(c, 55) if C else None
                if C: c_normed(c)
                if A: copy_values(a); means(a)
                if C: c_normed2(c)
                if C: depthwise(c, csteps)
                if C: silus(c, csteps)
                if A: block_queries(a)
                if Bb: normed(b, 1, "ln1_g", "ln1_b", bsteps)
                if A: row_max(a, 0)
                if A and more: copy_places(a + 1)
                if A: spread_chunk(a, 0)
                if C: softplus(c, csteps)
                if A: row_max(a, 1); copy_probs(a, 0)
                if Bb: rectify(b, 0)
                if C: softplus2(c, csteps)
                if A: row_max(a, 2); copy_probs(a, 1); spread_chunk(a, 1)
                if Bb: rectify(b, 1)
                if C: decays(c, csteps)
                if A: row_max(a, 3); copy_probs(a, 2); spread_chunk(a, 2)
                if C: decays2(c, csteps)
                if A: row_max(a, 4); copy_probs(a, 3); spread_chunk(a, 3)
                if Bb: rectify(b, 2)
                if C: mask_gram(c)
                if C: scaled(c)
                if A: row_max(a, 5); copy_probs(a, 4); spread_chunk(a, 4); spread_chunk(a, 5)
                if A: row_max(a, 6); copy_probs(a, 5); spread_chunk(a, 6)
                if Bb: rectify(b, 3)
                if C: scan_out(c, csteps)
                if A: row_max(a, 7); copy_probs(a, 6); spread_chunk(a, 7)
                if C: block_out(c, csteps)
                if A: row_max(a, 8); copy_probs(a, 7); spread_chunk(a, 8)
                if A: row_max(a, 9); copy_probs(a, 8); spread_chunk(a, 9)
                if C: c_normed3(c)
                if A: copy_probs(a, 9)
                if Bb: normed(b, 2, "ln2_g", "ln2_b", bsteps)
                if C: route(c, csteps)
                if C: route2(c, csteps)
                if A: block_rows(a, Steps(a, 3, before=2))
                if Bb: fuse(b)
                if C: queue(c, csteps)
                if C: own_rows(c, csteps)
                if A: z_rows(a)
                if Bb: pool_half(b, 0, bsteps)
                if A: z_rest(a)
                if Bb: pool_half(b, 1, bsteps)
                if C: base_rows(c, csteps)
                if A: z_low(a)
                if C: experts(c, 0, csteps)
                if A: residual(a)
                if A and more: take_mean(a + 1, Steps(a + 1, 3))
                if C: experts(c, 1, csteps)
                if C: experts(c, 2, csteps)
                for steps in (bsteps, csteps):
                    if steps:
                        steps.end()

            copy_places(0)
            take_mean(0, Steps(0, 3))
            turns(turn, dve)


_NAMES = {"q_w": "tok", "q_b": "tok", "k_w": "tok", "k_b": "tok", "v_w": "tok", "v_b": "tok", "o_w": "tok",
          "o_b": "tok", "ln1_g": "tok", "ln1_b": "tok", "f1_w": "tok", "f1_b": "tok", "f2_w": "tok",
          "f2_b": "tok", "ln2_g": "tok", "ln2_b": "tok", "conv_w": "tok", "conv_b": "tok",
          "norm_w": "attn", "W_in": "attn", "W_dt": "attn", "b_dt": "attn", "W_B": "attn",
          "W_C": "attn", "W_out": "attn", "log_A": "attn", "D_param": "attn", "W_ffn1": "attn",
          "W_ffn2": "attn", "W_merge": "attn",
          "switch_w": "ffn", "switch_b": "ffn", "expert_w": "ffn", "expert_b": "ffn"}
_INS = {short: f"L0_{block}_{short}" for short, block in _NAMES.items()}
_INS["aconv_w"] = "L0_attn_conv_w"
_INS["aconv_b"] = "L0_attn_conv_b"


def kernel(**inputs):
    import numpy as _np
    import concourse.bacc as _bacc
    from concourse import mybir as _mybir
    from concourse.bass_utils import run_bass_kernel_spmd as _run

    nc = _bacc.Bacc("TRN2", target_bir_lowering=False, num_devices=1)
    arrays, handles = {}, {}
    for short, name in [("x", "x"), *_INS.items()]:
        a = _np.ascontiguousarray(inputs[name])
        arrays[f"in_{name}"] = a
        handles[short] = nc.dram_tensor(f"in_{name}", a.shape, _mybir.dt.from_np(a.dtype), kind="ExternalInput").ap()
    out = nc.dram_tensor("out_0", (B, T, D), _mybir.dt.float32, kind="ExternalOutput").ap()
    build(nc, handles.pop("x"), handles, out)
    r = _run(nc, [arrays], core_ids=[0])
    return r.results[0]["out_0"]
```
